# Optimizing a Trainium2 kernel written in Bass

```python
import numpy as np
import jax
import jax.numpy as jnp

def _softmax(x, axis=-1):
    return jax.nn.softmax(x, axis=axis)

def _gelu(x):
    return jax.nn.gelu(x, approximate=True)

def _silu(x):
    return jax.nn.silu(x)

def _sigmoid(x):
    return jax.nn.sigmoid(x)

def _layernorm(x, axis=-1, eps=1e-05):
    m = jnp.mean(x, axis=axis, keepdims=True)
    v = jnp.var(x, axis=axis, keepdims=True)
    return (x - m) / jnp.sqrt(v + eps)

def _scatter_add(tgt, idx, src, axis=0):
    return tgt.at[idx].add(src)

def _segment_sum(src, seg, n):
    return jax.ops.segment_sum(src, seg, n)
kernel_name = 'mk_decoder_postln_d1_seqx_r4_0ceccb'

def setup_inputs(seed: int=0):
    np.random.seed(seed)
    _w = jnp.asarray

    def _rec_inputs():
        import jax
        import jax.numpy as jnp
        _rk = jax.random.key(seed)
        x = 7.22e-05 + 1 * jax.random.normal(jax.random.fold_in(_rk, 1), (32, 256, 256), jnp.float32)
        _lenS = 256 - jax.random.randint(jax.random.fold_in(_rk, 7), (32,), 0, max(1, 256 // 4) + 1, jnp.int32)
        _lenS2 = 256 - jax.random.randint(jax.random.fold_in(_rk, 8), (32,), 0, max(1, 256 // 4) + 1, jnp.int32)
        _ctx_1024P = jax.random.normal(jax.random.fold_in(_rk, 11), (32, 16, 256), jnp.float32)
        _ctx_1024c = jax.random.dirichlet(jax.random.fold_in(_rk, 511), 0.3 * jnp.ones((16,), jnp.float32), (32, 256))
        _ctx_1024t = jnp.einsum('bsk,bkd->bsd', _ctx_1024c, _ctx_1024P)
        _ctx_1024t = _ctx_1024t * jax.lax.rsqrt(jnp.mean(jnp.square(_ctx_1024t)) + 1e-12) * 0.953939
        ctx_1024 = 4.13588e-05 + 0.999923 * (_ctx_1024t + 0.3 * jax.random.normal(jax.random.fold_in(_rk, 611), (32, 256, 256), jnp.float32))
        itok_Bx1xSx1_0_63 = jax.random.randint(jax.random.fold_in(_rk, 12), (32, 1, 256, 1), 0, 64, jnp.int32)
        return (x, ctx_1024, itok_Bx1xSx1_0_63)
    x, ctx_1024, itok_Bx1xSx1_0_63 = _rec_inputs()

    def _L0_attn_setup():
        import jax, jax.numpy as jnp
        import numpy as np
        import math
        B, L, D = (2, 512, 256)
        H, KV, HD = (16, 4, 64)
        GROUPS = H // KV
        ROPE_BASE = 10000.0

        def _alibi_slopes(n_heads):

            def pow2(n):
                start = 2.0 ** (-2.0 ** (-(math.log2(n) - 3)))
                return [start * start ** i for i in range(n)]
            if math.log2(n_heads).is_integer():
                return pow2(n_heads)
            c = 2 ** math.floor(math.log2(n_heads))
            return pow2(c) + _alibi_slopes(2 * c)[0::2][:n_heads - c]

        def _rope_cos_sin(seq_len, dim, dtype):
            inv_freq = 1.0 / ROPE_BASE ** (jnp.arange(0, dim, 2, dtype=jnp.float32) / dim)
            t = jnp.arange(seq_len, dtype=jnp.float32)
            freqs = t[:, None] * inv_freq[None, :]
            emb = jnp.concatenate([freqs, freqs], axis=-1)
            return (jnp.cos(emb).astype(dtype), jnp.sin(emb).astype(dtype))

        def _rotate_half(x):
            x1, x2 = (x[..., :x.shape[-1] // 2], x[..., x.shape[-1] // 2:])
            return jnp.concatenate([-x2, x1], axis=-1)
        key = jax.random.key(seed)
        ks = jax.random.split(key, 5)
        s = 0.02
        return {'x': jax.random.normal(ks[0], (B, L, D), jnp.float32), 'Wq': jax.random.normal(ks[1], (D, H * HD), jnp.float32) * s, 'Wk': jax.random.normal(ks[2], (D, KV * HD), jnp.float32) * s, 'Wv': jax.random.normal(ks[3], (D, KV * HD), jnp.float32) * s, 'Wo': jax.random.normal(ks[4], (H * HD, D), jnp.float32) * s}
    _L0_attn_all = _L0_attn_setup()
    _L0_attn_in = {k: v for k, v in _L0_attn_all.items() if k in ('Wq', 'Wk', 'Wv', 'Wo')}
    del _L0_attn_all

    def _L0_xattn_setup():
        import jax, jax.numpy as jnp
        import numpy as np
        HEADS = 16
        WINDOW = 64
        D_MODEL = 256

        def _ln(x, g, b, eps=1e-05):
            m = jnp.mean(x, -1, keepdims=True)
            var = jnp.mean((x - m) ** 2, -1, keepdims=True)
            return (x - m) * jax.lax.rsqrt(var + eps) * g + b

        def _proj(x, g, b, W, bias):
            return _ln(x, g, b) @ W.T + bias

        def _bucket(x, pad_value):
            L = x.shape[-2]
            n = WINDOW * -(-L // WINDOW)
            pads = [(0, 0)] * x.ndim
            pads[-2] = (0, n - L)
            x = jnp.pad(x, pads, constant_values=pad_value)
            return x.reshape(*x.shape[:-2], n // WINDOW, WINDOW, x.shape[-1])

        def _unfold(x, pad_value):
            pads = [(0, 0)] * x.ndim
            pads[-3] = (1, 0)
            prev = jnp.pad(x, pads, constant_values=pad_value)[..., :-1, :, :]
            return jnp.concatenate([prev, x], axis=-2)

        def _rotary(x):
            S, d = (x.shape[-2], x.shape[-1])
            inv = 1.0 / 10000.0 ** (jnp.arange(0, d, 2, dtype=jnp.float32) / d)
            freqs = jnp.arange(S, dtype=jnp.float32)[:, None] * inv[None, :]
            freqs = jnp.repeat(freqs, 2, axis=-1)
            cos, sin = (jnp.cos(freqs).astype(x.dtype), jnp.sin(freqs).astype(x.dtype))
            xp = x.reshape(*x.shape[:-1], d // 2, 2)
            xr = jnp.stack([-xp[..., 1], xp[..., 0]], axis=-1).reshape(x.shape)
            return x * cos + xr * sin

        def _forward(q, k, v, cell, ln_q_w, ln_q_b, w_q, b_q, ln_k_w, ln_k_b, w_k, b_k, ln_v_w, ln_v_b, w_v, b_v, ln_o_w, ln_o_b, w_o, b_o):
            B, L, D = q.shape
            hd = D // HEADS

            def split_heads(x):
                return x.reshape(B, L, HEADS, hd).transpose(0, 2, 1, 3)
            qh = split_heads(_proj(q, ln_q_w, ln_q_b, w_q, b_q))
            kh = split_heads(_proj(k, ln_k_w, ln_k_b, w_k, b_k))
            vh = split_heads(_proj(v, ln_v_w, ln_v_b, w_v, b_v))
            bq = _bucket(qh, -1.0)
            bk = _unfold(_bucket(kh, -1.0), -1.0)
            bv = _unfold(_bucket(vh, -1.0), -1.0)
            nb = bq.shape[2]
            n = nb * WINDOW
            i = _bucket(jnp.arange(n, dtype=jnp.int32)[:, None], -1)
            j = jnp.swapaxes(_unfold(i, -1), -1, -2)
            mask = (i >= j) & (j != -1)
            req = _bucket(cell, -1)
            rek = jnp.swapaxes(_unfold(req, -1), -1, -2)
            mask = mask & (req == rek)
            bq = _rotary(bq)
            bk = _rotary(bk)
            p = jnp.einsum('bhnqd,bhnkd->bhnqk', bq, bk) / jnp.sqrt(jnp.asarray(hd, bq.dtype))
            p = jnp.where(mask, p, jnp.finfo(p.dtype).min)
            a = jax.nn.softmax(p, axis=-1)
            o = jnp.einsum('bhnqk,bhnkd->bhnqd', a, bv)
            o = o.reshape(B, HEADS, n, hd)[:, :, :L]
            o = o.transpose(0, 2, 1, 3).reshape(B, L, D)
            return _proj(o, ln_o_w, ln_o_b, w_o, b_o)
        key = jax.random.key(seed)
        ks = jax.random.split(key, 10)
        B, L, D = (2, 1024, D_MODEL)
        inp = {'q': jax.random.normal(ks[0], (B, L, D), dtype=jnp.float32), 'k': jax.random.normal(ks[1], (B, L, D), dtype=jnp.float32), 'v': jax.random.normal(ks[2], (B, L, D), dtype=jnp.float32), 'cell': jnp.sort(jax.random.randint(ks[3], (B, 1, L, 1), 0, 64, dtype=jnp.int32), axis=2)}
        for idx, name in enumerate(['q', 'k', 'v', 'o']):
            inp[f'ln_{name}_w'] = jnp.ones((D,), jnp.float32)
            inp[f'ln_{name}_b'] = jnp.zeros((D,), jnp.float32)
            inp[f'w_{name}'] = jax.random.normal(ks[4 + idx], (D, D), dtype=jnp.float32) * 0.02
            inp[f'b_{name}'] = jnp.zeros((D,), jnp.float32)
        return inp
    _L0_xattn_all = _L0_xattn_setup()
    _L0_xattn_in = {k: v for k, v in _L0_xattn_all.items() if k in ('ln_q_w', 'ln_q_b', 'w_q', 'b_q', 'ln_k_w', 'ln_k_b', 'w_k', 'b_k', 'ln_v_w', 'ln_v_b', 'w_v', 'b_v', 'ln_o_w', 'ln_o_b', 'w_o', 'b_o')}
    del _L0_xattn_all

    def _L0_ffn_setup():
        import jax, jax.numpy as jnp
        import numpy as np
        HIDDEN = 256
        INNER = 1024

        def _weight_quant(w):
            scale = 1.0 / jnp.clip(jnp.mean(jnp.abs(w)), 1e-05)
            wq = jnp.clip(jnp.round(w * scale), -1.0, 1.0) / scale
            return w + jax.lax.stop_gradient(wq - w)

        def _act_quant(x):
            scale = 127.0 / jnp.clip(jnp.max(jnp.abs(x), axis=-1, keepdims=True), 1e-05)
            xq = jnp.clip(jnp.round(x * scale), -128.0, 127.0) / scale
            return x + jax.lax.stop_gradient(xq - x)

        def _bitlinear(x, w):
            return jnp.einsum('bsi,oi->bso', _act_quant(x), _weight_quant(w))
        key = jax.random.key(seed)
        k0, k1, k2, k3 = jax.random.split(key, 4)
        x = jax.random.normal(k0, (4, 512, HIDDEN), dtype=jnp.float32)
        w_gate = jax.random.normal(k1, (INNER, HIDDEN), dtype=jnp.float32) / np.sqrt(HIDDEN)
        w_up = jax.random.normal(k2, (INNER, HIDDEN), dtype=jnp.float32) / np.sqrt(HIDDEN)
        w_down = jax.random.normal(k3, (HIDDEN, INNER), dtype=jnp.float32) / np.sqrt(INNER)
        return {'x': x, 'w_gate': w_gate, 'w_up': w_up, 'w_down': w_down}
    _L0_ffn_all = _L0_ffn_setup()
    _L0_ffn_in = {k: v for k, v in _L0_ffn_all.items() if k in ('w_gate', 'w_up', 'w_down')}
    del _L0_ffn_all
    return {'x': x, 'ctx_1024': ctx_1024, 'itok_Bx1xSx1_0_63': itok_Bx1xSx1_0_63, 'L0_attn_Wq': _L0_attn_in['Wq'], 'L0_attn_Wk': _L0_attn_in['Wk'], 'L0_attn_Wv': _L0_attn_in['Wv'], 'L0_attn_Wo': _L0_attn_in['Wo'], 'L0_xattn_ln_q_w': _L0_xattn_in['ln_q_w'], 'L0_xattn_ln_q_b': _L0_xattn_in['ln_q_b'], 'L0_xattn_w_q': _L0_xattn_in['w_q'], 'L0_xattn_b_q': _L0_xattn_in['b_q'], 'L0_xattn_ln_k_w': _L0_xattn_in['ln_k_w'], 'L0_xattn_ln_k_b': _L0_xattn_in['ln_k_b'], 'L0_xattn_w_k': _L0_xattn_in['w_k'], 'L0_xattn_b_k': _L0_xattn_in['b_k'], 'L0_xattn_ln_v_w': _L0_xattn_in['ln_v_w'], 'L0_xattn_ln_v_b': _L0_xattn_in['ln_v_b'], 'L0_xattn_w_v': _L0_xattn_in['w_v'], 'L0_xattn_b_v': _L0_xattn_in['b_v'], 'L0_xattn_ln_o_w': _L0_xattn_in['ln_o_w'], 'L0_xattn_ln_o_b': _L0_xattn_in['ln_o_b'], 'L0_xattn_w_o': _L0_xattn_in['w_o'], 'L0_xattn_b_o': _L0_xattn_in['b_o'], 'L0_ffn_w_gate': _L0_ffn_in['w_gate'], 'L0_ffn_w_up': _L0_ffn_in['w_up'], 'L0_ffn_w_down': _L0_ffn_in['w_down']}

def reference(x, ctx_1024, itok_Bx1xSx1_0_63, L0_attn_Wq, L0_attn_Wk, L0_attn_Wv, L0_attn_Wo, L0_xattn_ln_q_w, L0_xattn_ln_q_b, L0_xattn_w_q, L0_xattn_b_q, L0_xattn_ln_k_w, L0_xattn_ln_k_b, L0_xattn_w_k, L0_xattn_b_k, L0_xattn_ln_v_w, L0_xattn_ln_v_b, L0_xattn_w_v, L0_xattn_b_v, L0_xattn_ln_o_w, L0_xattn_ln_o_b, L0_xattn_w_o, L0_xattn_b_o, L0_ffn_w_gate, L0_ffn_w_up, L0_ffn_w_down):
    import jax
    import jax.numpy as jnp

    def _L0_attn_ref(x, Wq, Wk, Wv, Wo):
        import jax, jax.numpy as jnp
        import numpy as np
        import math
        B, L, D = (2, 512, 256)
        H, KV, HD = (16, 4, 64)
        GROUPS = H // KV
        ROPE_BASE = 10000.0

        def _alibi_slopes(n_heads):

            def pow2(n):
                start = 2.0 ** (-2.0 ** (-(math.log2(n) - 3)))
                return [start * start ** i for i in range(n)]
            if math.log2(n_heads).is_integer():
                return pow2(n_heads)
            c = 2 ** math.floor(math.log2(n_heads))
            return pow2(c) + _alibi_slopes(2 * c)[0::2][:n_heads - c]

        def _rope_cos_sin(seq_len, dim, dtype):
            inv_freq = 1.0 / ROPE_BASE ** (jnp.arange(0, dim, 2, dtype=jnp.float32) / dim)
            t = jnp.arange(seq_len, dtype=jnp.float32)
            freqs = t[:, None] * inv_freq[None, :]
            emb = jnp.concatenate([freqs, freqs], axis=-1)
            return (jnp.cos(emb).astype(dtype), jnp.sin(emb).astype(dtype))

        def _rotate_half(x):
            x1, x2 = (x[..., :x.shape[-1] // 2], x[..., x.shape[-1] // 2:])
            return jnp.concatenate([-x2, x1], axis=-1)
        b, l, _ = x.shape
        q = (x @ Wq).reshape(b, l, H, HD).transpose(0, 2, 1, 3)
        k = (x @ Wk).reshape(b, l, KV, HD).transpose(0, 2, 1, 3)
        v = (x @ Wv).reshape(b, l, KV, HD).transpose(0, 2, 1, 3)
        k = jnp.repeat(k, GROUPS, axis=1)
        v = jnp.repeat(v, GROUPS, axis=1)
        cos, sin = _rope_cos_sin(l, HD, x.dtype)
        q = q * cos + _rotate_half(q) * sin
        k = k * cos + _rotate_half(k) * sin
        attn = jnp.einsum('bhqd,bhkd->bhqk', q, k) / math.sqrt(HD)
        pos = jnp.arange(l)
        rel = (pos[None, :] - pos[:, None]).astype(x.dtype)
        slopes = jnp.asarray(_alibi_slopes(H), dtype=x.dtype)
        attn = attn + slopes[None, :, None, None] * rel[None, None, :, :]
        attn = jax.nn.softmax(attn, axis=-1)
        out = jnp.einsum('bhqk,bhkd->bhqd', attn, v)
        out = out.transpose(0, 2, 1, 3).reshape(b, l, H * HD)
        return out @ Wo

    def _L0_xattn_ref(q, k, v, cell, ln_q_w, ln_q_b, w_q, b_q, ln_k_w, ln_k_b, w_k, b_k, ln_v_w, ln_v_b, w_v, b_v, ln_o_w, ln_o_b, w_o, b_o):
        import jax, jax.numpy as jnp
        import numpy as np
        HEADS = 16
        WINDOW = 64
        D_MODEL = 256

        def _ln(x, g, b, eps=1e-05):
            m = jnp.mean(x, -1, keepdims=True)
            var = jnp.mean((x - m) ** 2, -1, keepdims=True)
            return (x - m) * jax.lax.rsqrt(var + eps) * g + b

        def _proj(x, g, b, W, bias):
            return _ln(x, g, b) @ W.T + bias

        def _bucket(x, pad_value):
            L = x.shape[-2]
            n = WINDOW * -(-L // WINDOW)
            pads = [(0, 0)] * x.ndim
            pads[-2] = (0, n - L)
            x = jnp.pad(x, pads, constant_values=pad_value)
            return x.reshape(*x.shape[:-2], n // WINDOW, WINDOW, x.shape[-1])

        def _unfold(x, pad_value):
            pads = [(0, 0)] * x.ndim
            pads[-3] = (1, 0)
            prev = jnp.pad(x, pads, constant_values=pad_value)[..., :-1, :, :]
            return jnp.concatenate([prev, x], axis=-2)

        def _rotary(x):
            S, d = (x.shape[-2], x.shape[-1])
            inv = 1.0 / 10000.0 ** (jnp.arange(0, d, 2, dtype=jnp.float32) / d)
            freqs = jnp.arange(S, dtype=jnp.float32)[:, None] * inv[None, :]
            freqs = jnp.repeat(freqs, 2, axis=-1)
            cos, sin = (jnp.cos(freqs).astype(x.dtype), jnp.sin(freqs).astype(x.dtype))
            xp = x.reshape(*x.shape[:-1], d // 2, 2)
            xr = jnp.stack([-xp[..., 1], xp[..., 0]], axis=-1).reshape(x.shape)
            return x * cos + xr * sin

        def _forward(q, k, v, cell, ln_q_w, ln_q_b, w_q, b_q, ln_k_w, ln_k_b, w_k, b_k, ln_v_w, ln_v_b, w_v, b_v, ln_o_w, ln_o_b, w_o, b_o):
            B, L, D = q.shape
            hd = D // HEADS

            def split_heads(x):
                return x.reshape(B, L, HEADS, hd).transpose(0, 2, 1, 3)
            qh = split_heads(_proj(q, ln_q_w, ln_q_b, w_q, b_q))
            kh = split_heads(_proj(k, ln_k_w, ln_k_b, w_k, b_k))
            vh = split_heads(_proj(v, ln_v_w, ln_v_b, w_v, b_v))
            bq = _bucket(qh, -1.0)
            bk = _unfold(_bucket(kh, -1.0), -1.0)
            bv = _unfold(_bucket(vh, -1.0), -1.0)
            nb = bq.shape[2]
            n = nb * WINDOW
            i = _bucket(jnp.arange(n, dtype=jnp.int32)[:, None], -1)
            j = jnp.swapaxes(_unfold(i, -1), -1, -2)
            mask = (i >= j) & (j != -1)
            req = _bucket(cell, -1)
            rek = jnp.swapaxes(_unfold(req, -1), -1, -2)
            mask = mask & (req == rek)
            bq = _rotary(bq)
            bk = _rotary(bk)
            p = jnp.einsum('bhnqd,bhnkd->bhnqk', bq, bk) / jnp.sqrt(jnp.asarray(hd, bq.dtype))
            p = jnp.where(mask, p, jnp.finfo(p.dtype).min)
            a = jax.nn.softmax(p, axis=-1)
            o = jnp.einsum('bhnqk,bhnkd->bhnqd', a, bv)
            o = o.reshape(B, HEADS, n, hd)[:, :, :L]
            o = o.transpose(0, 2, 1, 3).reshape(B, L, D)
            return _proj(o, ln_o_w, ln_o_b, w_o, b_o)
        return _forward(q, k, v, cell, ln_q_w, ln_q_b, w_q, b_q, ln_k_w, ln_k_b, w_k, b_k, ln_v_w, ln_v_b, w_v, b_v, ln_o_w, ln_o_b, w_o, b_o)

    def _L0_ffn_ref(x, w_gate, w_up, w_down):
        import jax, jax.numpy as jnp
        import numpy as np
        HIDDEN = 256
        INNER = 1024

        def _weight_quant(w):
            scale = 1.0 / jnp.clip(jnp.mean(jnp.abs(w)), 1e-05)
            wq = jnp.clip(jnp.round(w * scale), -1.0, 1.0) / scale
            return w + jax.lax.stop_gradient(wq - w)

        def _act_quant(x):
            scale = 127.0 / jnp.clip(jnp.max(jnp.abs(x), axis=-1, keepdims=True), 1e-05)
            xq = jnp.clip(jnp.round(x * scale), -128.0, 127.0) / scale
            return x + jax.lax.stop_gradient(xq - x)

        def _bitlinear(x, w):
            return jnp.einsum('bsi,oi->bso', _act_quant(x), _weight_quant(w))
        gate = jax.nn.silu(_bitlinear(x, w_gate))
        up = _bitlinear(x, w_up)
        return _bitlinear(gate * up, w_down)
    x = _layernorm(x + _L0_attn_ref(x, L0_attn_Wq, L0_attn_Wk, L0_attn_Wv, L0_attn_Wo), axis=-1)
    x = _layernorm(x + _L0_xattn_ref(x, ctx_1024, ctx_1024, itok_Bx1xSx1_0_63, L0_xattn_ln_q_w, L0_xattn_ln_q_b, L0_xattn_w_q, L0_xattn_b_q, L0_xattn_ln_k_w, L0_xattn_ln_k_b, L0_xattn_w_k, L0_xattn_b_k, L0_xattn_ln_v_w, L0_xattn_ln_v_b, L0_xattn_w_v, L0_xattn_b_v, L0_xattn_ln_o_w, L0_xattn_ln_o_b, L0_xattn_w_o, L0_xattn_b_o), axis=-1)
    x = _layernorm(x + _L0_ffn_ref(x, L0_ffn_w_gate, L0_ffn_w_up, L0_ffn_w_down), axis=-1)
    return x

_drawn_inputs = setup_inputs


def setup_inputs(seed=0):
    import zlib

    import numpy as np

    out = dict(_drawn_inputs(seed))
    spreads = {'L0_xattn_ln_q_w': (1.0, 0.6),
     'L0_xattn_ln_q_b': (0.0, 0.8),
     'L0_xattn_b_q': (0.0, 0.8),
     'L0_xattn_ln_k_w': (1.0, 0.6),
     'L0_xattn_ln_k_b': (0.0, 0.8),
     'L0_xattn_b_k': (0.0, 0.8),
     'L0_xattn_ln_v_w': (1.0, 0.2),
     'L0_xattn_ln_v_b': (0.0, 0.1),
     'L0_xattn_b_v': (0.0, 0.1),
     'L0_xattn_ln_o_w': (1.0, 0.2),
     'L0_xattn_ln_o_b': (0.0, 0.1),
     'L0_xattn_b_o': (0.0, 0.1)}
    factors = {'L0_attn_Wq': 8.0, 'L0_attn_Wk': 8.0, 'L0_xattn_w_q': 3.74, 'L0_xattn_w_k': 3.717}
    for name, (base, spread) in spreads.items():
        noise = np.random.default_rng([zlib.crc32(name.encode()), seed]).standard_normal(out[name].shape)
        drawn = base * np.exp(spread * noise) if base else spread * noise
        out[name] = jnp.asarray(drawn.astype(out[name].dtype))
    for name, factor in factors.items():
        out[name] = (out[name] * factor).astype(out[name].dtype)
    return out
```

```python
from contextlib import ExitStack

import numpy as np

import concourse.bass as bass
from concourse import mybir

ALU = mybir.AluOpType
ACT = mybir.ActivationFunctionType
F32 = mybir.dt.float32
BF16 = mybir.dt.bfloat16
F32R = mybir.dt.float32r
I32 = mybir.dt.int32
AX_X = mybir.AxisListType.X

P = 128
B, L, D = 32, 256, 256
TT = L // P
KT = D // P
H, KV, HD = 16, 4, 64
PAIRS = H // 2
XH, XD = 16, 16
WIN = 64
XT = 4
K1 = L - WIN
INNER = 1024
IC = INNER // P
MAGIC = 12582912.0
BIG = 1.0e30
EPS = 1e-5
CREDIT = 2

COUNT = dict(
    xT_loaded=16, xtok_loaded=16, ctx_loaded=16, cell_loaded=32, stored=16,
    proj_mm=6, kT_mm=4, qT_mm=8, S_mm=16, T_mm=16, O_mm=8, W_mm=1,
    x_hi=1, x_lo=1, v_new=2, v_ready=1, rot_prod=18, rot_sum=6, rot_hi=6, rot_lo=6, k_ready=4, q_ready=8,
    s_neg=32, p_exp=32, p_recip=16, p_norm=16, pT_ready=16, oT_ready=8, y_ready=1,
    ln_stats=10, ln_mv=10, ln_eps=5, ln_rstd=5, ctx_stats=2, ctx_mv=2, ctx_eps=1, ctx_rstd=1, x1_ready=2, x1b_ready=1, nc_ready=2, nx_ready=2, no_ready=2,
    x2_ready=2, out_ready=2,
    C_mm=1, NX_mm=1, KV_mm=2, QX_mm=1, KXT_mm=1, QXT_mm=1, SX0_mm=4, SX1_mm=8, TX0_mm=4, TX1_mm=8,
    OX_mm=4, BX_mm=2, NO_mm=1, PO_mm=1,
    cellq_ready=1, pen_ready=2, mask_ready=2, cT_ready=1, nT_ready=1, kx_raw=2, vx_ready=2, qx_raw=1,
    turned=4, cosine=2, kx_rot=1, qx_rot=1, kxT_ready=1, qxT_ready=1, kx_ready=4,
    sx0_neg=16, sx1_neg=16, px0_exp=16, px1_exp=16, pTx0_ready=4, pTx1_ready=8, ox_ready=4,
    sx_recip=2, o_ready=2, noT_ready=1, y2_ready=1,
    XQ_mm=1, G_mm=4, U_mm=4, HT_mm=2, D_mm=1, quant_x=6, xq_shift=2, xq_ready=1, xs_tanh=1, xs_half=1,
    xqT_ready=1, tanh_ready=4, gate_ready=4, h_ready=4, quant_h=10, hq_shift=2, hq_ready=2, hqT_ready=2, y3_ready=2,
)
LN_Y, LN_X1, LN_O, LN_Y2, LN_Y3, LN_CTX = range(6)

BANKS = dict(S=(0, 1), T=2, proj=3, kT=4, qT=4, O=4, W=4, SX=5, G=5, TX=6, U=6, chain=7)


BODY = [
    ('y_stats',), ('S', 0, 0), ('y_apply',), ('qT', 2), ('S', 0, 1), ('x1_apply',), ('S', 1, 0), ('NX',), ('S', 1, 1),
    ('QX',), ('T', 0, 0), ('qT', 3), ('q_turn',), ('S', 2, 0), ('ctx_stats',), ('T', 0, 1), ('S', 2, 1), ('O', 0),
    ('QXT',), ('T', 1, 0), ('SX0', 0), ('T', 1, 1), ('SX1', 0, 0), ('proj', 0, 2), ('SX1', 0, 1), ('SX0', 1),
    ('TX0', 0), ('KX', 2), ('T', 2, 0), ('TX1', 0, 0), ('SX1', 1, 0), ('proj', 1, 2), ('SX1', 1, 1), ('TX1', 0, 1),
    ('S', 3, 0), ('TX0', 1), ('X',), ('qT', 4), ('OX', 0), ('S', 3, 1), ('TX1', 1, 0), ('SX0', 2), ('T', 2, 1),
    ('TX1', 1, 1), ('O', 1), ('KX', 3), ('SX1', 2, 0), ('TX0', 2), ('T', 3, 0), ('OX', 1), ('TX1', 2, 0), ('qT', 5),
    ('SX1', 2, 1), ('SX0', 3), ('S', 4, 0), ('TX1', 2, 1), ('SX1', 3, 0), ('S', 4, 1), ('SX1', 3, 1), ('proj', 0, 0),
    ('TX0', 3), ('O', 2), ('TX1', 3, 0), ('S', 5, 0), ('mask',), ('OX', 2), ('TX1', 3, 1), ('ctx_apply',), ('qT', 6),
    ('T', 3, 1), ('OX', 3), ('S', 5, 1), ('T', 4, 0), ('BX', 0), ('O', 3), ('BX', 1), ('o_stats',), ('S', 6, 0),
    ('qT', 7), ('C',), ('o_apply',), ('T', 4, 1), ('proj', 1, 0), ('NO',), ('S', 6, 1), ('PO',), ('y2_stats',),
    ('T', 5, 0), ('KV', 0), ('proj', 0, 1), ('y2_apply',), ('KV', 1), ('T', 5, 1), ('XQ',), ('G', 0, 0), ('O', 4),
    ('k_turn',), ('U', 0, 0), ('S', 7, 0), ('G', 0, 1), ('proj', 1, 1), ('O', 5), ('T', 6, 0), ('S', 7, 1), ('KXT',),
    ('U', 0, 1), ('kT', 0), ('T', 6, 1), ('G', 1, 0), ('kT', 1), ('U', 1, 0), ('T', 7, 0), ('G', 1, 1), ('O', 6),
    ('KX', 0), ('U', 1, 1), ('kT', 2), ('T', 7, 1), ('kT', 3), ('qT', 0), ('HT', 0), ('O', 7), ('HT', 1), ('D',),
    ('V',), ('y3_stats',), ('qT', 1), ('KX', 1), ('W',), ('y3_apply',),
]

SELF = ("X", "proj", "kT", "qT", "S", "T", "O", "V", "W")
KEYS = ("ctx_stats", "ctx_apply", "C", "KV", "k_turn", "mask", "KXT")


def of_self(step):
    return step[0] in SELF


def of_head(step):
    return step[0] in ("X", "kT", "V") or (step[0] == "proj" and step[2] < 2) or (step[0] == "qT" and step[1] < 2)


def of_keys(step):
    return step[0] in KEYS or (step[0] == "KX" and step[1] < 2)


STEPS = dict(
    first=[x for x in BODY if of_head(x) or of_keys(x)],
    second=[x for x in BODY if of_self(x)],
    body=BODY,
    next_to_last=[x for x in BODY if not of_head(x)],
    last=[x for x in BODY if not of_self(x) and not of_keys(x)],
)


def at(name, batch, k=0):
    return (batch + CREDIT) * COUNT[name] + (k + 1)


def landed(name, batch):
    return (batch + CREDIT + 1) * COUNT[name]


def build(nc, a, out):
    with ExitStack() as ctx:
        def sb(name, shape, dt=F32):
            return ctx.enter_context(nc.sbuf_tensor(name, shape, dt))

        sem = {name: ctx.enter_context(nc.semaphore(name)) for name in COUNT}
        proj_loaded = ctx.enter_context(nc.semaphore("proj_loaded"))
        weights_loaded = ctx.enter_context(nc.semaphore("weights_loaded"))
        pool_consts = ctx.enter_context(nc.semaphore("pool_consts"))
        pre_dve = ctx.enter_context(nc.semaphore("pre_dve"))
        waits_passed = ctx.enter_context(nc.semaphore("waits_passed"))
        pre_pe = ctx.enter_context(nc.semaphore("pre_pe"))

        psum = [ctx.enter_context(nc.psum_tensor(f"bank{i}", [P, 512], F32)) for i in range(8)]

        QKV = (2 * KV + H) * HD
        w_hi = sb("w_hi", [P, KT, QKV], F32R)
        w_lo = sb("w_lo", [P, KT, QKV], F32R)
        wo = sb("wo", [P, PAIRS, D])
        rope = sb("rope", [P, 2, TT, HD])
        alibi = sb("alibi", [P, 2, L])
        wqx = sb("wqx", [P, KT, D])
        wkvx = sb("wkvx", [P, KT, 2 * D])
        wox = sb("wox", [P, KT, D])
        ropex = sb("ropex", [P, 2, 2, TT, XD])
        pen0 = sb("pen0", [P, P])
        pen1 = sb("pen1", [P, K1])
        gb = sb("gb", [P, 8, KT])
        brow = sb("brow", [P, 4, D])
        wg16 = sb("wg16", [P, KT, INNER], BF16)
        wu16 = sb("wu16", [P, KT, INNER], BF16)
        wd16 = sb("wd16", [P, IC, D], BF16)
        ident = sb("ident", [P, P])
        ident16 = sb("ident16", [P, P], BF16)
        wsum = sb("wsum", [P, 3])
        wmean = sb("wmean", [P, 3])
        wrec = sb("wrec", [P, 3])
        wk1 = sb("wk1", [P, 3])

        xT = sb("xT", [P, KT, L])
        x_hi = sb("x_hi", [P, KT, L], F32R)
        x_lo = sb("x_lo", [P, KT, L], F32R)
        xtok = sb("xtok", [P, TT, D])
        ctxt = sb("ctxt", [P, TT, D])
        cellk = sb("cellk", [P, L], I32)
        cellq = sb("cellq", [P, TT], I32)
        cellqf = sb("cellqf", [P, TT])
        v_new = sb("v_new", [P, TT, KV * HD])
        v_sb = sb("v_sb", [P, TT, KV * HD])
        rot = sb("rot", [P, 2, 2, 512])
        ktok = sb("ktok", [P, TT, KV, 3 * HD], F32R)
        qtok = sb("qtok", [P, TT, 8, 2 * HD], F32R)
        kk = sb("kk", [P, 2, KV, L], F32R)
        qq = sb("qq", [P, 3, 2, L], F32R)
        prob = sb("prob", [P, 4, 2, L])
        nmax = sb("nmax", [P, 2 * H])
        psums = sb("psums", [P, 2 * H])
        precs = sb("precs", [P, 2 * H])
        pT = sb("pT", [P, 2, 2, TT, L])
        oT = sb("oT", [P, PAIRS, L])
        bn = sb("bn", [P, 6, TT, 6])
        mv = sb("mv", [P, 6, TT, 2])
        own_head = sb("own_head", [P, 8])
        veps = sb("veps", [P, 6, TT])
        rstd = sb("rstd", [P, 6, TT])
        minus_half = sb("minus_half", [P, TT])
        x1 = sb("x1", [P, TT, D])
        y = x1
        nx = sb("nx", [P, TT, D])
        nT = sb("nT", [P, KT, L])
        ncx = ctxt
        cT = sb("cT", [P, KT, L])
        mask0 = sb("mask0", [P, P])
        mask1 = sb("mask1", [P, K1])
        pm0, pm1 = mask0, mask1
        kxT = sb("kxT", [P, 2, L])
        kx = sb("kx", [P, 2, 4, L])
        vx = sb("vx", [P, TT, XH, 32])
        qx = cT
        px0 = sb("px0", [P, 2, 4, P])
        px1 = sb("px1", [P, 3, 2, L])
        nmx = sb("nmx", [P, TT, XH])
        sumx = sb("sumx", [P, TT, XH])
        recx = sb("recx", [P, TT, XH])
        pTx = sb("pTx", [P, 2, 4, 3, P])
        ox = sb("ox", [P, XT, L])
        n_o, noT = nx, nT
        y2 = sb("y2", [P, TT, D])
        o_tok = y2
        x2 = sb("x2", [P, TT, D])
        amx = sb("amx", [P, TT])
        ax = sb("ax", [P, 7, TT])
        xqT = sb("xqT", [P, KT, L], BF16)
        hh = sb("hh", [P, TT, INNER])
        xshift = hh[:, 0, 0:TT * D].rearrange("p (t n) -> p t n", t=TT)
        hs = sb("hs", [P, 6, TT])
        hq = sb("hq", [P, INNER], BF16)
        xq = hq[:, 0:TT * D].rearrange("p (t n) -> p t n", t=TT)
        hqT = sb("hqT", [P, TT, IC, P], BF16)
        y3 = y2
        out_sb = ox[:, 0:TT, :]
        kx_tok, qx_tok = nx, x2
        turn = [pTx[:].rearrange("p s h c n -> p (s h c n)")[:, 0:4 * D].rearrange("p (c t n) -> p c t n", c=2, t=TT),
                hh[:, 0, :].rearrange("p (c t n) -> p c t n", c=2, t=TT)]

        stage = [prob[:].rearrange("p s c n -> p (s c n)"), oT[:].rearrange("p h n -> p (h n)"),
                 pTx[:, 0:2, :, :, :].rearrange("p t h c n -> p (t h c n)")[:, 0:2048]]
        raw_w = [hh[:].rearrange("p t n -> p (t n)")[:, 0:QKV], pT[:].rearrange("p s c k n -> p (s c k n)")[:, 0:QKV]]
        ones = qx[:, 0, 0:P]
        bwide = px0[:].rearrange("p c h n -> p (c h n)").rearrange("p (c k n) -> p c k n", c=4, k=KT)

        LN = [y, x1, o_tok, y2, y3]

        first_loads = [
            (raw_w[0], a["wqkv"][0:P, :]), (raw_w[1], a["wqkv"][P:2 * P, :]),
            (rope[:].rearrange("p c t n -> p (c t n)"), a["rope"]),
        ]
        flat_loads = [
            (alibi[:].rearrange("p h n -> p (h n)"), a["alibi"]),
            (stage[0].rearrange("p (k n) -> p k n", k=KT), a["wg"].rearrange("(k p) n -> p k n", p=P)),
            (stage[1].rearrange("p (k n) -> p k n", k=KT), a["wu"].rearrange("(k p) n -> p k n", p=P)),
            (stage[2].rearrange("p (k n) -> p k n", k=IC), a["wd"].rearrange("(k p) n -> p k n", p=P)),
            (wo[:], a["wo"].rearrange("(k p) n -> p k n", p=P)),
            (wqx[:], a["wqx"].rearrange("(k p) n -> p k n", p=P)),
            (wkvx[:], a["wkvx"].rearrange("(k p) n -> p k n", p=P)),
            (wox[:], a["wox"].rearrange("(k p) n -> p k n", p=P)),
            (ropex[:].rearrange("p a c t n -> p (a c t n)"), a["ropex"]),
            (own_head[:], a["own_head"]), (pen0[:], a["pen0"]), (pen1[:], a["pen1"]),
            (gb[:].rearrange("p c k -> p (c k)"), a["gb"]),
        ] + [(brow[:, n, :], a["b_" + c].rearrange("(a n) -> a n", a=1).to_broadcast([P, D])) for n, c in enumerate("qkvo")]
        N_LOADS = 16 * len(flat_loads)

        xT_dram = a["xT"].rearrange("(k p) t -> p k t", p=P)
        x_dram = a["x"].rearrange("(b t p) d -> b p t d", t=TT, p=P)
        ctx_dram = a["ctx"].rearrange("(b t p) d -> b p t d", t=TT, p=P)
        cell_cols = a["cell"].rearrange("(b t p) -> b p t", t=TT, p=P)
        cell_rows = a["cell"].rearrange("(b t) -> b t", t=L)
        out_dram = out.rearrange("(b t p) d -> b p t d", t=TT, p=P)

        PRE_DVE = 35
        POOL_CONSTS = 8

        block = ctx.enter_context(nc.Block())

        @block.sync
        def _(sp):
            for name, n in COUNT.items():
                sp.sem_inc(sem[name], CREDIT * n)

            def one(ap, b):
                return ap[bass.ds(b, 1)]

            def load_ctx(b):
                sp.wait_ge(sem["C_mm"], at("C_mm", b - 1))
                sp.dma_start(ctxt[:], one(ctx_dram, b).rearrange("a p t d -> (a p) t d")).then_inc(sem["ctx_loaded"], 16)
                sp.wait_ge(sem["pen_ready"], at("pen_ready", b - 1, 1))
                sp.dma_start(cellq[:], one(cell_cols, b).rearrange("a p t -> (a p) t"),
                             allow_slow_non_contiguous=True).then_inc(sem["cell_loaded"], 16)
                sp.dma_start(cellk[:], one(cell_rows, b).to_broadcast([P, L])).then_inc(sem["cell_loaded"], 16)

            def load_xT(b):
                sp.wait_ge(sem["x_hi"], at("x_hi", b - 1))
                sp.wait_ge(sem["x_lo"], at("x_lo", b - 1))
                sp.dma_start(xT[:], xT_dram[:, :, bass.ds(b * L, L)]).then_inc(sem["xT_loaded"], 16)

            def load_xtok(b):
                sp.wait_ge(sem["y_ready"], at("y_ready", b - 1))
                sp.dma_start(xtok[:], one(x_dram, b).rearrange("a p t d -> (a p) t d")).then_inc(sem["xtok_loaded"], 16)

            def store(b):
                sp.wait_ge(sem["out_ready"], at("out_ready", b, 1))
                sp.dma_start(one(out_dram, b).rearrange("a p t d -> (a p) t d"), out_sb).then_inc(sem["stored"], 16)

            load_xT(0)
            for dst, src in first_loads:
                sp.dma_start(dst, src).then_inc(proj_loaded, 16)
            for dst, src in flat_loads:
                sp.dma_start(dst, src).then_inc(weights_loaded, 16)
            load_xtok(0)
            load_ctx(0)
            load_xT(1)
            load_ctx(1)
            load_xtok(1)
            load_xT(2)
            with sp.Fori(0, B - 3) as j:
                load_ctx(j + 2)
                load_xtok(j + 2)
                load_xT(j + 3)
                store(j)
            load_ctx(B - 1)
            load_xtok(B - 1)
            store(B - 3)
            store(B - 2)
            store(B - 1)
            sp.wait_ge(sem["stored"], landed("stored", B - 1))

        @block.tensor
        def _(pe):
            mm = nc.tensor.matmul

            def transposes(bank, blocks):
                for n, src in enumerate(blocks):
                    last = nc.tensor.transpose(bank[:, n * P:(n + 1) * P], src, ident[:])
                return last

            def transposes_r(bank, blocks):
                for n, src in enumerate(blocks):
                    last = nc.tensor.transpose(bank[:, n * P:(n + 1) * P], src.bitcast(F32), ident[:])
                return last

            def transposes16(bank, blocks):
                for n, src in enumerate(blocks):
                    last = nc.tensor.transpose(bank[:].bitcast(BF16)[:, n * P:(n + 1) * P], src, ident16[:])
                return last

            def run(phase, bm, br):
                head = phase in ("second", "body")
                bh = 0 if phase == "first" else bm + 1 if head else None
                ahead = phase in ("first", "body", "next_to_last")
                bk = 0 if phase == "first" else br + 1 if ahead else None
                for step in STEPS[phase]:
                    kind, args = step[0], step[1:]
                    if kind == "proj":
                        t, c = args
                        b = bm if c == 2 else bh
                        if c < 2 and t == 0:
                            pe.wait_ge(sem["x_hi"], at("x_hi", b))
                            pe.wait_ge(sem["x_lo"], at("x_lo", b))
                        if (t, c) == (0, 0):
                            pe.wait_ge(sem["rot_prod"], at("rot_prod", b - 1, 17))
                        else:
                            pe.wait_ge(sem["rot_prod"], at("rot_prod", b, 3 * (2 * c + t) - 1))
                        if (t, c) in ((1, 0), (0, 1)):
                            pe.wait_ge(sem["v_new"], at("v_new", b, 2 * c + t - 1))
                        parts = ((x_hi, w_hi), (x_lo, w_hi), (x_hi, w_lo))
                        for i in range(KT * 3):
                            k, (xs, ws) = i // 3, parts[i % 3]
                            last = mm(psum[BANKS["proj"]][:], xs[:, k, t * P:(t + 1) * P], ws[:, k, c * 512:(c + 1) * 512],
                                      start=i == 0, stop=i == KT * 3 - 1)
                        last.then_inc(sem["proj_mm"], 1)
                    elif kind == "kT":
                        i, = args
                        t, h = i % 2, i // 2
                        pe.wait_ge(sem["rot_lo"], at("rot_lo", bh, t))
                        if i == 0:
                            pe.wait_ge(sem["oT_ready"], at("oT_ready", bh - 1, PAIRS - 3))
                        elif i == 1:
                            pe.wait_ge(sem["k_ready"], at("k_ready", bh, 0))
                        elif i == 2:
                            pe.wait_ge(sem["k_ready"], at("k_ready", bh, 1))
                            pe.wait_ge(sem["oT_ready"], at("oT_ready", bh - 1, PAIRS - 2))
                        else:
                            pe.wait_ge(sem["k_ready"], at("k_ready", bh, 2))
                        transposes_r(psum[BANKS["kT"]], [ktok[:, t, g, c * HD:c * HD + P] for g in (2 * h, 2 * h + 1) for c in range(2)])\
                            .then_inc(sem["kT_mm"], 1)
                    elif kind == "qT":
                        p, = args
                        b = bh if p < 2 else bm
                        if p % 4 == 0:
                            pe.wait_ge(sem["rot_lo"], at("rot_lo", b, 3 if p < 4 else 5))
                        if p == 0:
                            pe.wait_ge(sem["k_ready"], at("k_ready", b, 3))
                        elif p == 1:
                            pe.wait_ge(sem["q_ready"], at("q_ready", b, 0))
                            pe.wait_ge(sem["oT_ready"], at("oT_ready", b - 1, PAIRS - 1))
                        elif p == 2:
                            pe.wait_ge(sem["y_ready"], at("y_ready", b - 1))
                            pe.wait_ge(sem["q_ready"], at("q_ready", b, 1))
                        elif p == 3:
                            pe.wait_ge(sem["q_ready"], at("q_ready", b, 2))
                        else:
                            pe.wait_ge(sem["oT_ready"], at("oT_ready", b, p - 4))
                        transposes_r(psum[BANKS["qT"]], [qtok[:, t, 2 * (p % 4) + c, :] for c in range(2) for t in range(TT)])\
                            .then_inc(sem["qT_mm"], 1)
                    elif kind == "S":
                        p, q = args
                        n = 2 * p + q
                        if q == 0:
                            pe.wait_ge(sem["q_ready"], at("q_ready", bm, p))
                        if n == 0:
                            pe.wait_ge(sem["k_ready"], at("k_ready", bm, 3))
                        pe.wait_ge(sem["s_neg"], at("s_neg", bm, 2 * n - 3))
                        for c in range(2):
                            for i in range(2):
                                last = mm(psum[BANKS["S"][n % 2]][:, c * L:(c + 1) * L], qq[:, p % 3, c, q * P:(q + 1) * P],
                                          kk[:, i, p // 2, :], start=i == 0, stop=i == 1)
                        last.then_inc(sem["S_mm"], 1)
                    elif kind == "T":
                        p, q = args
                        n = 2 * p + q
                        pe.wait_ge(sem["p_norm"], at("p_norm", bm, n))
                        pe.wait_ge(sem["pT_ready"], at("pT_ready", bm, n - 1))
                        transposes(psum[BANKS["T"]], [prob[:, n % 4, c, k * P:(k + 1) * P] for c in range(2) for k in range(TT)])\
                            .then_inc(sem["T_mm"], 1)
                    elif kind == "O":
                        p, = args
                        if p == 0:
                            pe.wait_ge(sem["v_ready"], at("v_ready", bm))
                        pe.wait_ge(sem["pT_ready"], at("pT_ready", bm, 2 * p + 1))
                        if p <= PAIRS - 4:
                            pe.wait_ge(sem["q_ready"], at("q_ready", bm, p + 3))
                        elif head and p == PAIRS - 2:
                            pe.wait_ge(sem["k_ready"], at("k_ready", bh, 1))
                        elif head and p == PAIRS - 1:
                            pe.wait_ge(sem["q_ready"], at("q_ready", bh, 0))
                        else:
                            pe.wait_ge(sem["oT_ready"], at("oT_ready", bm, p - 1))
                        for k in range(TT):
                            for c in range(2):
                                last = mm(psum[BANKS["O"]][c * HD:(c + 1) * HD, 0:L], v_sb[:, k, (p // 2) * HD:(p // 2 + 1) * HD],
                                          pT[:, p % 2, c, k, :], start=k == 0, stop=k == TT - 1)
                        last.then_inc(sem["O_mm"], 1)
                    elif kind == "W":
                        pe.wait_ge(sem["oT_ready"], at("oT_ready", bm, PAIRS - 1))
                        if head:
                            pe.wait_ge(sem["q_ready"], at("q_ready", bh, 1))
                        for t in range(TT):
                            for k in range(PAIRS):
                                last = mm(psum[BANKS["W"]][:, t * D:(t + 1) * D], oT[:, k, t * P:(t + 1) * P], wo[:, k, :],
                                          start=k == 0, stop=k == PAIRS - 1)
                        last.then_inc(sem["W_mm"], 1)
                    elif kind == "C":
                        pe.wait_ge(sem["nc_ready"], at("nc_ready", bk, 1))
                        pe.wait_ge(sem["o_ready"], at("o_ready", bk - 1, 1))
                        transposes(psum[7], [ncx[:, t, k * P:(k + 1) * P] for k in range(KT) for t in range(TT)]).then_inc(sem["C_mm"], 1)
                    elif kind == "NX":
                        pe.wait_ge(sem["nx_ready"], at("nx_ready", br, 1))
                        pe.wait_ge(sem["y3_ready"], at("y3_ready", br - 1, 1))
                        transposes(psum[7], [nx[:, t, k * P:(k + 1) * P] for k in range(KT) for t in range(TT)]).then_inc(sem["NX_mm"], 1)
                    elif kind == "NO":
                        pe.wait_ge(sem["no_ready"], at("no_ready", br, 1))
                        if ahead:
                            pe.wait_ge(sem["cT_ready"], at("cT_ready", bk))
                        transposes(psum[7], [n_o[:, t, k * P:(k + 1) * P] for k in range(KT) for t in range(TT)]).then_inc(sem["NO_mm"], 1)
                    elif kind == "KV":
                        t, = args
                        if t == 0:
                            pe.wait_ge(sem["cT_ready"], at("cT_ready", bk))
                            pe.wait_ge(sem["y2_ready"], at("y2_ready", bk - 1))
                        else:
                            pe.wait_ge(sem["kx_raw"], at("kx_raw", bk, 0))
                            pe.wait_ge(sem["vx_ready"], at("vx_ready", bk, 0))
                        for k in range(KT):
                            last = mm(psum[7][:], cT[:, k, t * P:(t + 1) * P], wkvx[:, k, :], start=k == 0, stop=k == KT - 1)
                        last.then_inc(sem["KV_mm"], 1)
                    elif kind == "QX":
                        pe.wait_ge(sem["nT_ready"], at("nT_ready", br))
                        for t in range(TT):
                            for k in range(KT):
                                last = mm(psum[7][:, t * D:(t + 1) * D], nT[:, k, t * P:(t + 1) * P], wqx[:, k, :],
                                          start=k == 0, stop=k == KT - 1)
                        last.then_inc(sem["QX_mm"], 1)
                    elif kind == "KXT":
                        pe.wait_ge(sem["kx_rot"], at("kx_rot", bk))
                        pe.wait_ge(sem["xqT_ready"], at("xqT_ready", bk - 1))
                        transposes(psum[7], [kx_tok[:, t, k * P:(k + 1) * P] for k in range(KT) for t in range(TT)])\
                            .then_inc(sem["KXT_mm"], 1)
                    elif kind == "QXT":
                        pe.wait_ge(sem["qx_rot"], at("qx_rot", br))
                        transposes(psum[7], [qx_tok[:, t, k * P:(k + 1) * P] for k in range(KT) for t in range(TT)])\
                            .then_inc(sem["QXT_mm"], 1)
                    elif kind == "SX0":
                        t, = args
                        pe.wait_ge(sem["kx_ready"], at("kx_ready", br, t))
                        if t == 0:
                            pe.wait_ge(sem["qxT_ready"], at("qxT_ready", br))
                            pe.wait_ge(sem["gate_ready"], at("gate_ready", br - 1, 3))
                        else:
                            pe.wait_ge(sem["sx1_neg"], at("sx1_neg", br, 4 * t - 1))
                        mm(psum[BANKS["SX"]][:].rearrange("p (h n) -> p h n", h=4), qx[:, t // 2, 0:P], kx[:, t % 2, :, 0:P],
                           start=True, stop=True).then_inc(sem["SX0_mm"], 1)
                    elif kind == "SX1":
                        t, h = args
                        if h == 0:
                            pe.wait_ge(sem["sx0_neg"], at("sx0_neg", br, 4 * t + 3))
                        else:
                            pe.wait_ge(sem["sx1_neg"], at("sx1_neg", br, 4 * t + 1))
                        mm(psum[BANKS["SX"]][:, 0:2 * K1].rearrange("p (h n) -> p h n", h=2), qx[:, t // 2, P:2 * P],
                           kx[:, t % 2, 2 * h:2 * h + 2, WIN:L], start=True, stop=True).then_inc(sem["SX1_mm"], 1)
                    elif kind == "TX0":
                        t, = args
                        pe.wait_ge(sem["px0_exp"], at("px0_exp", br, 4 * t + 3))
                        if t == 0:
                            pe.wait_ge(sem["h_ready"], at("h_ready", br - 1, 3))
                        else:
                            pe.wait_ge(sem["pTx1_ready"], at("pTx1_ready", br, 2 * t - 1))
                        transposes(psum[BANKS["TX"]], [px0[:, t % 2, h, :] for h in range(4)]).then_inc(sem["TX0_mm"], 1)
                    elif kind == "TX1":
                        t, h = args
                        n = 2 * t + h
                        pe.wait_ge(sem["px1_exp"], at("px1_exp", br, 2 * n + 1))
                        if h == 0:
                            pe.wait_ge(sem["pTx0_ready"], at("pTx0_ready", br, t))
                        else:
                            pe.wait_ge(sem["pTx1_ready"], at("pTx1_ready", br, n - 1))
                        transposes(psum[BANKS["TX"]], [px1[:, n % 3, c, k * P:(k + 1) * P] for c in range(2) for k in range(TT)])\
                            .then_inc(sem["TX1_mm"], 1)
                    elif kind == "OX":
                        t, = args
                        pe.wait_ge(sem["pTx1_ready"], at("pTx1_ready", br, 2 * t + 1))
                        if t:
                            pe.wait_ge(sem["ox_ready"], at("ox_ready", br, t - 1))
                        else:
                            pe.wait_ge(sem["vx_ready"], at("vx_ready", br, 1))
                        for blk, kt, first, last_ in ((0, 0, True, True), (1, 0, True, False), (2, 1, False, True)):
                            col = P if blk else 0
                            for h in range(4):
                                last = mm(psum[7][32 * h:32 * h + 32, col:col + P], vx[:, kt, 4 * t + h, :],
                                          pTx[:, t % 2, h, blk, :], start=first, stop=last_)
                        last.then_inc(sem["OX_mm"], 1)
                    elif kind == "BX":
                        q, = args
                        if q == 0:
                            pe.wait_ge(sem["ox_ready"], at("ox_ready", br, 3))
                        else:
                            pe.wait_ge(sem["o_ready"], at("o_ready", br, 0))
                        transposes(psum[7], [ox[:, t, q * P:(q + 1) * P] for t in range(XT)]).then_inc(sem["BX_mm"], 1)
                    elif kind == "PO":
                        pe.wait_ge(sem["noT_ready"], at("noT_ready", br))
                        for t in range(TT):
                            for k in range(KT):
                                last = mm(psum[7][:, t * D:(t + 1) * D], noT[:, k, t * P:(t + 1) * P], wox[:, k, :],
                                          start=k == 0, stop=k == KT - 1)
                        last.then_inc(sem["PO_mm"], 1)
                    elif kind == "XQ":
                        pe.wait_ge(sem["xq_ready"], at("xq_ready", br))
                        if ahead:
                            pe.wait_ge(sem["kx_raw"], at("kx_raw", bk, 1))
                            pe.wait_ge(sem["vx_ready"], at("vx_ready", bk, 1))
                        transposes16(psum[7], [xq[:, t, k * P:(k + 1) * P] for k in range(KT) for t in range(TT)])\
                            .then_inc(sem["XQ_mm"], 1)
                    elif kind == "G":
                        t, c = args
                        if (t, c) == (0, 0):
                            pe.wait_ge(sem["xqT_ready"], at("xqT_ready", br))
                            pe.wait_ge(sem["sx1_neg"], at("sx1_neg", br, 15))
                        else:
                            pe.wait_ge(sem["gate_ready"], at("gate_ready", br, 2 * t + c - 1))
                        for k in range(KT):
                            last = mm(psum[BANKS["G"]][:], xqT[:, k, t * P:(t + 1) * P], wg16[:, k, c * 512:(c + 1) * 512],
                                      start=k == 0, stop=k == KT - 1)
                        last.then_inc(sem["G_mm"], 1)
                    elif kind == "U":
                        t, c = args
                        if (t, c) == (0, 0):
                            pe.wait_ge(sem["pTx1_ready"], at("pTx1_ready", br, 7))
                        else:
                            pe.wait_ge(sem["h_ready"], at("h_ready", br, 2 * t + c - 1))
                        for k in range(KT):
                            last = mm(psum[BANKS["U"]][:], xqT[:, k, t * P:(t + 1) * P], wu16[:, k, c * 512:(c + 1) * 512],
                                      start=k == 0, stop=k == KT - 1)
                        last.then_inc(sem["U_mm"], 1)
                    elif kind == "HT":
                        t, = args
                        pe.wait_ge(sem["hq_ready"], at("hq_ready", br, t))
                        if t:
                            pe.wait_ge(sem["hqT_ready"], at("hqT_ready", br, 0))
                        elif ahead:
                            pe.wait_ge(sem["kxT_ready"], at("kxT_ready", bk))
                        transposes16(psum[7], [hq[:, k * P:(k + 1) * P] for k in range(IC)]).then_inc(sem["HT_mm"], 1)
                    elif kind == "D":
                        pe.wait_ge(sem["hqT_ready"], at("hqT_ready", br, 1))
                        for t in range(TT):
                            for k in range(IC):
                                last = mm(psum[7][:, t * D:(t + 1) * D], hqT[:, t, k, :], wd16[:, k, :],
                                          start=k == 0, stop=k == IC - 1)
                        last.then_inc(sem["D_mm"], 1)

            pe.wait_ge(weights_loaded, N_LOADS)
            pe.wait_ge(pool_consts, POOL_CONSTS)
            pe.wait_ge(pre_dve, 11)
            for n, w in enumerate((wqx, wkvx[:, :, 0:D], wkvx[:, :, D:2 * D], wox)):
                for k in range(KT):
                    mm(psum[1 + n // 2][:, (n % 2) * D:(n % 2 + 1) * D], bwide[:, n, k, :], w[:, k, :], start=k == 0, stop=k == KT - 1)
            mm(psum[0][:, 0:3], ones, wsum[:], start=True, stop=True).then_inc(pre_pe, 1)
            pe.wait_ge(pre_dve, PRE_DVE)
            run("first", None, None)
            run("second", 0, None)
            with pe.Fori(0, B - 2) as j:
                run("body", j + 1, j)
            run("next_to_last", B - 1, B - 2)
            run("last", None, B - 1)

        @block.vector
        def _(dve):
            v = nc.vector

            def ln_stats(n, b):
                for t in range(TT):
                    v.bn_stats(bn[:, n, t, :], LN[n][:, t, :]).then_inc(sem["ln_stats"], 1)
                for t in range(TT):
                    dve.wait_ge(sem["ln_stats"], at("ln_stats", b, 2 * n + t))
                    dve.sem_inc(waits_passed, 1)
                    v.bn_aggr(mv[:, n, t, :], bn[:, n, t, :]).then_inc(sem["ln_mv"], 1)

            def ln_apply(n, b, dst, done):
                dve.wait_ge(sem["ln_rstd"], at("ln_rstd", b, n))
                for t in range(TT):
                    v.tensor_scalar(dst[:, t, :], LN[n][:, t, :], mv[:, n, t, 0:1], rstd[:, n, t:t + 1],
                                    ALU.subtract, ALU.mult).then_inc(done, 1)

            def recip_of(b, n):
                dve.wait_ge(sem["p_exp"], at("p_exp", b, 2 * n + 1))
                v.reciprocal(precs[:, 2 * n:2 * n + 2], psums[:, 2 * n:2 * n + 2]).then_inc(sem["p_recip"], 1)

            def turn_x(n, src, b):
                sine = ropex[:, n, 1, :, :].unsqueeze(2).to_broadcast([P, TT, XH, XD])
                four = src[:].rearrange("p t (h d) -> p t h d", h=XH)
                dst = turn[n][:, 1, :, :].rearrange("p t (h d) -> p t h d", h=XH)
                for odd in range(2):
                    v.tensor_tensor(dst[:, :, :, odd::2], four[:, :, :, 1 - odd::2], sine[:, :, :, odd::2], ALU.mult)\
                        .then_inc(sem["turned"], 1)

            def quant_h(b, t):
                dve.wait_ge(sem["h_ready"], at("h_ready", b, 2 * t + 1))
                v.tensor_reduce(hs[:, 0, t:t + 1], hh[:, t, :], AX_X, ALU.max, apply_absolute_value=True).then_inc(sem["quant_h"], 1)
                dve.wait_ge(sem["quant_h"], at("quant_h", b, 5 * t))
                v.tensor_scalar(hs[:, 1, t:t + 1], hs[:, 0, t:t + 1], ax[:, 6, t:t + 1], EPS, ALU.mult, ALU.max).then_inc(sem["quant_h"], 1)
                dve.wait_ge(sem["quant_h"], at("quant_h", b, 5 * t + 1))
                v.reciprocal(hs[:, 2, t:t + 1], hs[:, 1, t:t + 1]).then_inc(sem["quant_h"], 1)
                dve.wait_ge(sem["quant_h"], at("quant_h", b, 5 * t + 2))
                v.tensor_scalar(hs[:, 3, t:t + 1], hs[:, 2, t:t + 1], 127.0, ax[:, 6, t:t + 1], ALU.mult, ALU.mult).then_inc(sem["quant_h"], 1)
                dve.wait_ge(sem["quant_h"], at("quant_h", b, 5 * t + 3))
                v.tensor_scalar(hh[:, t, :], hh[:, t, :], hs[:, 3, t:t + 1], MAGIC, ALU.mult, ALU.add).then_inc(sem["hq_shift"], 1)
                v.tensor_scalar(hs[:, 5, t:t + 1], hs[:, 1, t:t + 1], 1.0 / 127.0, wk1[:, 2:3], ALU.mult, ALU.mult).then_inc(sem["quant_h"], 1)
                dve.wait_ge(sem["hq_shift"], at("hq_shift", b, t))
                dve.wait_ge(sem["HT_mm"], at("HT_mm", b, t - 1))
                v.tensor_scalar(hq[:], hh[:, t, :], MAGIC, 127.0, ALU.subtract, ALU.min).then_inc(sem["hq_ready"], 1)

            def run(phase, bm, br):
                head = phase in ("second", "body")
                bh = 0 if phase == "first" else bm + 1 if head else None
                ahead = phase in ("first", "body", "next_to_last")
                bk = 0 if phase == "first" else br + 1 if ahead else None
                for step in STEPS[phase]:
                    kind, args = step[0], step[1:]
                    if kind == "X":
                        dve.wait_ge(sem["x_hi"], at("x_hi", bh))
                        v.tensor_tensor(x_lo[:], xT[:], x_hi[:].bitcast(F32), ALU.subtract).then_inc(sem["x_lo"], 1)
                    elif kind == "proj":
                        t, c = args
                        b = bm if c == 2 else bh
                        n = 2 * c + t
                        heads = 8 if c else KV
                        bank = psum[BANKS["proj"]][:, 0:heads * HD].rearrange("p (h a n) -> p h a n", h=heads, a=2)
                        cosine = rope[:, 0, t:t + 1, :].to_broadcast([P, heads, HD])
                        sine = rope[:, 1, t:t + 1, :].to_broadcast([P, heads, HD])
                        by_cos = rot[:, n % 2, 0, 0:heads * HD].rearrange("p (h n) -> p h n", h=heads)
                        by_sin = rot[:, n % 2, 1, 0:heads * HD].rearrange("p (h n) -> p h n", h=heads)
                        dve.wait_ge(sem["proj_mm"], at("proj_mm", b, n))
                        dve.wait_ge(sem["rot_lo"], at("rot_lo", b, n - 2))
                        v.tensor_tensor(by_cos, psum[BANKS["proj"]][:, 0:heads * HD].rearrange("p (h n) -> p h n", h=heads), cosine,
                                        ALU.mult).then_inc(sem["rot_prod"], 1)
                        for a_ in range(2):
                            lo = a_ * HD // 2
                            v.tensor_tensor(by_sin[:, :, lo:lo + HD // 2], bank[:, :, 1 - a_, :], sine[:, :, lo:lo + HD // 2],
                                            ALU.mult).then_inc(sem["rot_prod"], 1)
                        if c == 0:
                            dve.wait_ge(sem["v_ready"], at("v_ready", b - 1))
                            v.tensor_copy(v_new[:, t, :], psum[BANKS["proj"]][:, KV * HD:2 * KV * HD]).then_inc(sem["v_new"], 1)
                    elif kind == "S":
                        p, q = args
                        n = 2 * p + q
                        dve.wait_ge(sem["S_mm"], at("S_mm", bm, n))
                        dve.sem_inc(waits_passed, 1)
                        for c in range(2):
                            v.tensor_tensor_reduce(out=prob[:, n % 4, c, :], in0=psum[BANKS["S"][n % 2]][:, c * L:(c + 1) * L],
                                                   in1=alibi[:, c, :], scale=-2.0 ** -p, scalar=3.0e38,
                                                   op0=ALU.add, op1=ALU.min, accum_out=nmax[:, 2 * n + c:2 * n + c + 1])\
                                .then_inc(sem["s_neg"], 1)
                        if n:
                            recip_of(bm, n - 1)
                    elif kind == "T":
                        p, q = args
                        if 2 * p + q == 2 * PAIRS - 2:
                            recip_of(bm, 2 * PAIRS - 1)
                    elif kind == "W":
                        dve.wait_ge(sem["xtok_loaded"], landed("xtok_loaded", bm))
                        dve.wait_ge(sem["W_mm"], at("W_mm", bm))
                        v.tensor_tensor(y[:], psum[BANKS["W"]][:].rearrange("p (t n) -> p t n", t=TT), xtok[:], ALU.add)\
                            .then_inc(sem["y_ready"], 1)
                    elif kind == "y_stats":
                        dve.wait_ge(sem["y_ready"], at("y_ready", br))
                        ln_stats(LN_Y, br)
                    elif kind == "ctx_stats":
                        dve.wait_ge(sem["ctx_loaded"], landed("ctx_loaded", bk))
                        for t in range(TT):
                            v.bn_stats(bn[:, LN_CTX, t, :], ctxt[:, t, :]).then_inc(sem["ctx_stats"], 1)
                        for t in range(TT):
                            dve.wait_ge(sem["ctx_stats"], at("ctx_stats", bk, t))
                            dve.sem_inc(waits_passed, 1)
                            v.bn_aggr(mv[:, LN_CTX, t, :], bn[:, LN_CTX, t, :]).then_inc(sem["ctx_mv"], 1)
                    elif kind == "y_apply":
                        ln_apply(LN_Y, br, x1, sem["x1_ready"])
                        dve.wait_ge(sem["x1_ready"], at("x1_ready", br, 1))
                        ln_stats(LN_X1, br)
                    elif kind == "ctx_apply":
                        dve.wait_ge(sem["ctx_rstd"], at("ctx_rstd", bk))
                        for t in range(TT):
                            v.tensor_scalar(ncx[:, t, :], ctxt[:, t, :], mv[:, LN_CTX, t, 0:1], rstd[:, LN_CTX, t:t + 1],
                                            ALU.subtract, ALU.mult).then_inc(sem["nc_ready"], 1)
                    elif kind == "x1_apply":
                        dve.wait_ge(sem["KXT_mm"], at("KXT_mm", br))
                        ln_apply(LN_X1, br, nx, sem["nx_ready"])
                    elif kind == "mask":
                        dve.wait_ge(sem["cell_loaded"], landed("cell_loaded", bk))
                        v.tensor_copy(cellqf[:], cellq[:]).then_inc(sem["cellq_ready"], 1)
                        dve.wait_ge(sem["cellq_ready"], at("cellq_ready", bk))
                        v.scalar_tensor_tensor(out=pm0[:], in0=cellk[:, 0:P], scalar=cellqf[:, 0:1], in1=pen0[:],
                                               op0=ALU.not_equal, op1=ALU.max).then_inc(sem["pen_ready"], 1)
                        v.scalar_tensor_tensor(out=pm1[:], in0=cellk[:, WIN:L], scalar=cellqf[:, 1:2], in1=pen1[:],
                                               op0=ALU.not_equal, op1=ALU.max).then_inc(sem["pen_ready"], 1)
                        dve.wait_ge(sem["pen_ready"], at("pen_ready", bk, 1))
                        v.tensor_scalar(mask0[:], pm0[:], -BIG, None, ALU.mult).then_inc(sem["mask_ready"], 1)
                        v.tensor_scalar(mask1[:], pm1[:], -BIG, None, ALU.mult).then_inc(sem["mask_ready"], 1)
                    elif kind == "KV":
                        t, = args
                        dve.wait_ge(sem["KV_mm"], at("KV_mm", bk, t))
                        v.tensor_tensor(kx_tok[:, t, :], psum[7][:, 0:D], brow[:, 1, :], ALU.add).then_inc(sem["kx_raw"], 1)
                        v.tensor_tensor(vx[:, t, :, 0:XD], psum[7][:, D:2 * D].rearrange("p (h n) -> p h n", h=XH),
                                        brow[:, 2, :].rearrange("p (h n) -> p h n", h=XH), ALU.add).then_inc(sem["vx_ready"], 1)
                    elif kind == "k_turn":
                        dve.wait_ge(sem["kx_raw"], at("kx_raw", bk, 1))
                        turn_x(0, kx_tok, bk)
                    elif kind == "QX":
                        dve.wait_ge(sem["QX_mm"], at("QX_mm", br))
                        v.tensor_tensor(qx_tok[:], psum[7][:].rearrange("p (t n) -> p t n", t=TT),
                                        brow[:, 0:1, :].to_broadcast([P, TT, D]), ALU.add).then_inc(sem["qx_raw"], 1)
                    elif kind == "q_turn":
                        dve.wait_ge(sem["qx_raw"], at("qx_raw", br))
                        turn_x(1, qx_tok, br)
                    elif kind == "SX0":
                        t, = args
                        if t == 0:
                            dve.wait_ge(sem["mask_ready"], at("mask_ready", br, 1))
                        dve.wait_ge(sem["SX0_mm"], at("SX0_mm", br, t))
                        dve.sem_inc(waits_passed, 1)
                        for h in range(4):
                            v.tensor_tensor_reduce(out=px0[:, t % 2, h, :], in0=psum[BANKS["SX"]][:, h * P:(h + 1) * P],
                                                   in1=mask0[:], scale=-1.0, scalar=3.0e38, op0=ALU.add, op1=ALU.min,
                                                   accum_out=nmx[:, 0, 4 * t + h:4 * t + h + 1]).then_inc(sem["sx0_neg"], 1)
                    elif kind == "SX1":
                        t, hf = args
                        n = 2 * t + hf
                        dve.wait_ge(sem["SX1_mm"], at("SX1_mm", br, n))
                        dve.sem_inc(waits_passed, 1)
                        for c in range(2):
                            h = 4 * t + 2 * hf + c
                            v.tensor_tensor_reduce(out=px1[:, n % 3, c, WIN:L], in0=psum[BANKS["SX"]][:, c * K1:(c + 1) * K1],
                                                   in1=mask1[:], scale=-1.0, scalar=3.0e38, op0=ALU.add, op1=ALU.min,
                                                   accum_out=nmx[:, 1, h:h + 1]).then_inc(sem["sx1_neg"], 1)
                    elif kind == "TX0":
                        t, = args
                        dve.wait_ge(sem["TX0_mm"], at("TX0_mm", br, t))
                        v.tensor_copy(pTx[:, t % 2, :, 0, :], psum[BANKS["TX"]][:].rearrange("p (h n) -> p h n", h=4))\
                            .then_inc(sem["pTx0_ready"], 1)
                    elif kind == "BX":
                        q, = args
                        if q == 0:
                            dve.wait_ge(sem["px0_exp"], at("px0_exp", br, 15))
                        else:
                            dve.wait_ge(sem["px1_exp"], at("px1_exp", br, 15))
                        v.reciprocal(recx[:, q, :], sumx[:, q, :]).then_inc(sem["sx_recip"], 1)
                        dve.wait_ge(sem["BX_mm"], at("BX_mm", br, q))
                        dve.wait_ge(sem["sx_recip"], at("sx_recip", br, q))
                        v.tensor_tensor(o_tok[:, q, :].rearrange("p (h n) -> p h n", h=XH),
                                        psum[7][:].rearrange("p (h n) -> p h n", h=XH)[:, :, 0:XD],
                                        recx[:, q, :].unsqueeze(2).to_broadcast([P, XH, XD]), ALU.mult)\
                            .then_inc(sem["o_ready"], 1)
                    elif kind == "o_stats":
                        dve.wait_ge(sem["o_ready"], at("o_ready", br, 1))
                        ln_stats(LN_O, br)
                    elif kind == "o_apply":
                        dve.wait_ge(sem["NX_mm"], at("NX_mm", br))
                        ln_apply(LN_O, br, n_o, sem["no_ready"])
                    elif kind == "PO":
                        dve.wait_ge(sem["PO_mm"], at("PO_mm", br))
                        dve.wait_ge(sem["x1b_ready"], at("x1b_ready", br))
                        v.tensor_tensor(y2[:], psum[7][:].rearrange("p (t n) -> p t n", t=TT), x1[:], ALU.add)\
                            .then_inc(sem["y2_ready"], 1)
                    elif kind == "y2_stats":
                        dve.wait_ge(sem["y2_ready"], at("y2_ready", br))
                        ln_stats(LN_Y2, br)
                    elif kind == "y2_apply":
                        ln_apply(LN_Y2, br, x2, sem["x2_ready"])
                    elif kind == "XQ":
                        dve.wait_ge(sem["x2_ready"], at("x2_ready", br, 1))
                        v.tensor_reduce(amx[:], x2[:], AX_X, ALU.max, apply_absolute_value=True).then_inc(sem["quant_x"], 1)
                        dve.wait_ge(sem["quant_x"], at("quant_x", br, 0))
                        v.tensor_scalar(ax[:, 0, :], amx[:], EPS, None, ALU.max).then_inc(sem["quant_x"], 1)
                        dve.wait_ge(sem["quant_x"], at("quant_x", br, 1))
                        v.reciprocal(ax[:, 1, :], ax[:, 0, :]).then_inc(sem["quant_x"], 1)
                        dve.wait_ge(sem["quant_x"], at("quant_x", br, 2))
                        v.tensor_scalar(ax[:, 2, :], ax[:, 1, :], 127.0, None, ALU.mult).then_inc(sem["quant_x"], 1)
                        dve.wait_ge(sem["quant_x"], at("quant_x", br, 3))
                        for t in range(TT):
                            v.tensor_scalar(xshift[:, t, :], x2[:, t, :], ax[:, 2, t:t + 1], MAGIC, ALU.mult, ALU.add)\
                                .then_inc(sem["xq_shift"], 1)
                        v.tensor_scalar(ax[:, 3, :], ax[:, 0, :], 1.0 / 127.0, None, ALU.mult).then_inc(sem["quant_x"], 1)
                        dve.wait_ge(sem["xq_shift"], at("xq_shift", br, 1))
                        dve.wait_ge(sem["HT_mm"], at("HT_mm", br - 1, 1))
                        v.tensor_scalar(xq, xshift, MAGIC, 127.0, ALU.subtract, ALU.min).then_inc(sem["xq_ready"], 1)
                        dve.wait_ge(sem["tanh_ready"], at("tanh_ready", br - 1, 3))
                        dve.wait_ge(sem["quant_x"], at("quant_x", br, 4))
                        v.tensor_scalar(ax[:, 4, :], ax[:, 3, :], wk1[:, 0:1], None, ALU.mult).then_inc(sem["xs_tanh"], 1)
                        v.tensor_tensor(ax[:, 5, :], ax[:, 3, :], ax[:, 3, :], ALU.mult).then_inc(sem["quant_x"], 1)
                        dve.wait_ge(sem["quant_x"], at("quant_x", br, 5))
                        v.tensor_scalar(ax[:, 6, :], ax[:, 5, :], wk1[:, 1:2], None, ALU.mult).then_inc(sem["xs_half"], 1)
                        dve.wait_ge(sem["XQ_mm"], at("XQ_mm", br))
                        dve.wait_ge(sem["U_mm"], at("U_mm", br - 1, 3))
                        v.tensor_scalar(xqT[:], psum[7][:].bitcast(BF16)[:, 0:KT * L].rearrange("p (k n) -> p k n", k=KT),
                                        -128.0, None, ALU.max).then_inc(sem["xqT_ready"], 1)
                    elif kind == "U":
                        t, c = args
                        n = 2 * t + c
                        part = hh[:, t, c * 512:(c + 1) * 512]
                        dve.wait_ge(sem["tanh_ready"], at("tanh_ready", br, n))
                        v.scalar_tensor_tensor(out=part, in0=part, scalar=1.0, in1=psum[BANKS["G"]][:], op0=ALU.add, op1=ALU.mult)\
                            .then_inc(sem["gate_ready"], 1)
                        dve.wait_ge(sem["gate_ready"], at("gate_ready", br, n))
                        dve.wait_ge(sem["U_mm"], at("U_mm", br, n))
                        v.tensor_tensor(part, part, psum[BANKS["U"]][:], ALU.mult).then_inc(sem["h_ready"], 1)
                        if c == 1:
                            quant_h(br, t)
                    elif kind == "HT":
                        t, = args
                        dve.wait_ge(sem["HT_mm"], at("HT_mm", br, t))
                        dve.wait_ge(sem["D_mm"], at("D_mm", br - 1))
                        v.tensor_scalar(hqT[:, t, :, :], psum[7][:].bitcast(BF16).rearrange("p (k n) -> p k n", k=IC),
                                        -128.0, None, ALU.max).then_inc(sem["hqT_ready"], 1)
                    elif kind == "D":
                        dve.wait_ge(sem["D_mm"], at("D_mm", br))
                        for t in range(TT):
                            v.scalar_tensor_tensor(out=y3[:, t, :], in0=psum[7][:, t * D:(t + 1) * D], scalar=hs[:, 5, t:t + 1],
                                                   in1=x2[:, t, :], op0=ALU.mult, op1=ALU.add).then_inc(sem["y3_ready"], 1)
                    elif kind == "y3_stats":
                        dve.wait_ge(sem["y3_ready"], at("y3_ready", br, 1))
                        ln_stats(LN_Y3, br)
                    elif kind == "y3_apply":
                        dve.wait_ge(sem["stored"], landed("stored", br - 1))
                        ln_apply(LN_Y3, br, out_sb, sem["out_ready"])

            dve.wait_ge(proj_loaded, 16 * len(first_loads))
            for k in range(KT):
                v.tensor_copy(w_hi[:, k, :], raw_w[k]).then_inc(pre_dve, 1)
            for k in range(KT):
                dve.wait_ge(pre_dve, k + 1)
                v.tensor_tensor(w_lo[:, k, :], raw_w[k], w_hi[:, k, :].bitcast(F32), ALU.subtract).then_inc(pre_dve, 1)
            dve.wait_ge(weights_loaded, N_LOADS)
            for n in range(4):
                v.tensor_copy(bwide[:, n, :, :], gb[:, 2 * n + 1, :].unsqueeze(2).to_broadcast([P, KT, P])).then_inc(pre_dve, 1)
            for n in range(3):
                v.tensor_reduce(wsum[:, n:n + 1], stage[n], AX_X, ALU.add, apply_absolute_value=True).then_inc(pre_dve, 1)
            dve.wait_ge(pre_pe, 1)
            for n in range(2):
                v.tensor_tensor(brow[:, 2 * n:2 * n + 2, :], psum[1 + n][:].rearrange("p (c n) -> p c n", c=2),
                                brow[:, 2 * n:2 * n + 2, :], ALU.add).then_inc(pre_dve, 1)
            for w, col in ((wqx, 0), (wkvx[:, :, 0:D], 2), (wkvx[:, :, D:2 * D], 4), (wox, 6)):
                for k in range(KT):
                    v.tensor_scalar(w[:, k, :], w[:, k, :], gb[:, col, k:k + 1], None, ALU.mult).then_inc(pre_dve, 1)
            v.tensor_scalar(wmean[:], psum[0][:, 0:3], 1.0 / (INNER * D), EPS, ALU.mult, ALU.max).then_inc(pre_dve, 1)
            dve.wait_ge(pre_dve, 22)
            v.reciprocal(wrec[:], wmean[:]).then_inc(pre_dve, 1)
            v.tensor_scalar(wk1[:, 0:1], wmean[:, 0:1], 0.5, None, ALU.mult).then_inc(pre_dve, 1)
            v.tensor_tensor(wk1[:, 2:3], wmean[:, 2:3], ones[:, 0:1], ALU.mult).then_inc(pre_dve, 1)
            dve.wait_ge(pre_dve, 25)
            v.tensor_tensor(wk1[:, 1:2], wk1[:, 0:1], wmean[:, 1:2], ALU.mult).then_inc(pre_dve, 1)
            for n in range(3):
                v.tensor_scalar(stage[n], stage[n], wrec[:, n:n + 1], MAGIC, ALU.mult, ALU.add).then_inc(pre_dve, 1)
            for n in range(3):
                dve.wait_ge(pre_dve, 27 + n)
                v.tensor_scalar(stage[n], stage[n], MAGIC, 1.0, ALU.subtract, ALU.min).then_inc(pre_dve, 1)
            for n, dst in enumerate((wg16, wu16, wd16)):
                dve.wait_ge(pre_dve, 30 + n)
                v.tensor_scalar(dst[:].rearrange("p k n -> p (k n)"), stage[n], -1.0, None, ALU.max).then_inc(pre_dve, 1)
            dve.wait_ge(pre_dve, PRE_DVE)
            dve.wait_ge(pool_consts, POOL_CONSTS)
            run("first", None, None)
            run("second", 0, None)
            with dve.Fori(0, B - 2) as j:
                run("body", j + 1, j)
            run("next_to_last", B - 1, B - 2)
            run("last", None, B - 1)

        @block.scalar
        def _(act):
            def run(phase, bm, br):
                head = phase in ("second", "body")
                bh = 0 if phase == "first" else bm + 1 if head else None
                ahead = phase in ("first", "body", "next_to_last")
                bk = 0 if phase == "first" else br + 1 if ahead else None
                for step in STEPS[phase]:
                    kind, args = step[0], step[1:]
                    if kind == "X":
                        act.wait_ge(sem["xT_loaded"], landed("xT_loaded", bh))
                        act.wait_ge(sem["proj_mm"], at("proj_mm", bh - 1, 5))
                        nc.scalar.copy(x_hi[:], xT[:]).then_inc(sem["x_hi"], 1)
                    elif kind == "proj":
                        t, c = args
                        b = bm if c == 2 else bh
                        n = 2 * c + t
                        act.wait_ge(sem["rot_sum"], at("rot_sum", b, n))
                        if c == 0:
                            nc.scalar.copy(ktok[:, t, :, :].rearrange("p g (a n) -> p g a n", a=3)[:, :, 0::2, :],
                                           rot[:, n % 2, 0, 0:KV * HD].rearrange("p (g a n) -> p g a n", g=KV, a=1)
                                           .to_broadcast([P, KV, 2, HD])).then_inc(sem["rot_hi"], 1)
                        else:
                            nc.scalar.copy(qtok[:, t, :, 0:HD], rot[:, n % 2, 0, :].rearrange("p (h n) -> p h n", h=8))\
                                .then_inc(sem["rot_hi"], 1)
                    elif kind == "kT":
                        i, = args
                        t, h = i % 2, i // 2
                        act.wait_ge(sem["kT_mm"], at("kT_mm", bh, i))
                        nc.scalar.copy(kk[:, :, 2 * h:2 * h + 2, t * P:(t + 1) * P].rearrange("p c g n -> p g c n"),
                                       psum[BANKS["kT"]][:].rearrange("p (g c n) -> p g c n", g=2, c=2)).then_inc(sem["k_ready"], 1)
                    elif kind == "qT":
                        p, = args
                        b = bh if p < 2 else bm
                        act.wait_ge(sem["qT_mm"], at("qT_mm", b, p))
                        nc.scalar.activation(qq[:, p % 3, :, :], psum[BANKS["qT"]][:].rearrange("p (c n) -> p c n", c=2), ACT.Copy,
                                             scale=2.0 ** p / 8.0).then_inc(sem["q_ready"], 1)
                    elif kind == "S":
                        p, q = args
                        n = 2 * p + q
                        for c in range(2):
                            i = 2 * n + c
                            act.wait_ge(sem["s_neg"], at("s_neg", bm, i))
                            nc.scalar.activation(prob[:, n % 4, c, :], prob[:, n % 4, c, :], ACT.Exp,
                                                 bias=nmax[:, i:i + 1], scale=-1.0, accum_out=psums[:, i:i + 1])\
                                .then_inc(sem["p_exp"], 1)
                    elif kind == "T":
                        p, q = args
                        act.wait_ge(sem["T_mm"], at("T_mm", bm, 2 * p + q))
                        nc.scalar.copy(pT[:, p % 2, :, :, q * P:(q + 1) * P].rearrange("p c k n -> p (c k) n"),
                                       psum[BANKS["T"]][:].rearrange("p (c n) -> p c n", c=4)).then_inc(sem["pT_ready"], 1)
                    elif kind == "O":
                        u, = args
                        act.wait_ge(sem["O_mm"], at("O_mm", bm, u))
                        nc.scalar.copy(oT[:, u, :], psum[BANKS["O"]][:, 0:L]).then_inc(sem["oT_ready"], 1)
                    elif kind == "C":
                        act.wait_ge(sem["C_mm"], at("C_mm", bk))
                        act.wait_ge(sem["KV_mm"], at("KV_mm", bk - 1, 1))
                        nc.scalar.copy(cT[:], psum[7][:].rearrange("p (k n) -> p k n", k=KT)).then_inc(sem["cT_ready"], 1)
                    elif kind == "NX":
                        act.wait_ge(sem["NX_mm"], at("NX_mm", br))
                        act.wait_ge(sem["PO_mm"], at("PO_mm", br - 1))
                        nc.scalar.copy(nT[:], psum[7][:].rearrange("p (k n) -> p k n", k=KT)).then_inc(sem["nT_ready"], 1)
                    elif kind == "NO":
                        act.wait_ge(sem["NO_mm"], at("NO_mm", br))
                        act.wait_ge(sem["QX_mm"], at("QX_mm", br))
                        nc.scalar.copy(noT[:], psum[7][:].rearrange("p (k n) -> p k n", k=KT)).then_inc(sem["noT_ready"], 1)
                    elif kind == "KXT":
                        act.wait_ge(sem["KXT_mm"], at("KXT_mm", bk))
                        act.wait_ge(sem["kx_ready"], at("kx_ready", bk - 1, 3))
                        nc.scalar.copy(kxT[:], psum[7][:].rearrange("p (k n) -> p k n", k=KT)).then_inc(sem["kxT_ready"], 1)
                    elif kind == "QXT":
                        act.wait_ge(sem["QXT_mm"], at("QXT_mm", br))
                        act.wait_ge(sem["SX1_mm"], at("SX1_mm", br - 1, 7))
                        nc.scalar.copy(qx[:], psum[7][:].rearrange("p (k n) -> p k n", k=KT)).then_inc(sem["qxT_ready"], 1)
                    elif kind == "SX0":
                        t, = args
                        if t == 0:
                            act.wait_ge(sem["sx_recip"], at("sx_recip", br - 1, 1))
                        for h in range(4):
                            i = 4 * t + h
                            act.wait_ge(sem["sx0_neg"], at("sx0_neg", br, i))
                            nc.scalar.activation(px0[:, t % 2, h, :], px0[:, t % 2, h, :], ACT.Exp, bias=nmx[:, 0, i:i + 1],
                                                 scale=-1.0, accum_out=sumx[:, 0, i:i + 1]).then_inc(sem["px0_exp"], 1)
                    elif kind == "SX1":
                        t, hf = args
                        n = 2 * t + hf
                        for c in range(2):
                            i = 2 * n + c
                            act.wait_ge(sem["sx1_neg"], at("sx1_neg", br, i))
                            nc.scalar.activation(px1[:, n % 3, c, WIN:L], px1[:, n % 3, c, WIN:L], ACT.Exp,
                                                 bias=nmx[:, 1, i:i + 1], scale=-1.0, accum_out=sumx[:, 1, i:i + 1])\
                                .then_inc(sem["px1_exp"], 1)
                    elif kind == "TX1":
                        t, hf = args
                        act.wait_ge(sem["TX1_mm"], at("TX1_mm", br, 2 * t + hf))
                        for c in range(2):
                            ins = nc.scalar.copy(pTx[:, t % 2, 2 * hf + c, 1:3, :],
                                                 psum[BANKS["TX"]][:, c * L:(c + 1) * L].rearrange("p (k n) -> p k n", k=TT))
                        ins.then_inc(sem["pTx1_ready"], 1)
                    elif kind == "OX":
                        u, = args
                        act.wait_ge(sem["OX_mm"], at("OX_mm", br, u))
                        if u == 0:
                            act.wait_ge(sem["stored"], landed("stored", br - 1))
                        nc.scalar.copy(ox[:, u, :], psum[7][:, 0:L]).then_inc(sem["ox_ready"], 1)
                    elif kind == "G":
                        t, c = args
                        n = 2 * t + c
                        if n == 0:
                            act.wait_ge(sem["xs_tanh"], at("xs_tanh", br))
                        act.wait_ge(sem["G_mm"], at("G_mm", br, n))
                        nc.scalar.activation(hh[:, t, c * 512:(c + 1) * 512], psum[BANKS["G"]][:], ACT.Tanh, scale=ax[:, 4, t:t + 1])\
                            .then_inc(sem["tanh_ready"], 1)

            run("first", None, None)
            run("second", 0, None)
            with act.Fori(0, B - 2) as j:
                run("body", j + 1, j)
            run("next_to_last", B - 1, B - 2)
            run("last", None, B - 1)

        @block.gpsimd
        def _(pool):
            g = nc.gpsimd

            def normalise(b, n):
                pool.wait_ge(sem["p_recip"], at("p_recip", b, n))
                g.tensor_tensor(prob[:, n % 4, :, :], prob[:, n % 4, :, :],
                                precs[:, 2 * n:2 * n + 2].unsqueeze(2).to_broadcast([P, 2, L]), ALU.mult)\
                    .then_inc(sem["p_norm"], 1)

            def ln_rstd(b, n):
                pool.wait_ge(sem["ln_mv"], at("ln_mv", b, 2 * n + 1))
                pool.sem_inc(waits_passed, 1)
                g.tensor_scalar(veps[:, n, :], mv[:, n, :, 1], EPS, None, ALU.add).then_inc(sem["ln_eps"], 1)
                pool.wait_ge(sem["ln_eps"], at("ln_eps", b, n))
                g.tensor_tensor(rstd[:, n, :], veps[:, n, :], minus_half[:], ALU.pow).then_inc(sem["ln_rstd"], 1)

            def cosine_x(n, src):
                for t in range(TT):
                    ins = g.tensor_tensor(turn[n][:, 0, t, :].rearrange("p (h d) -> p h d", h=XH), src[:, t, :].rearrange("p (h d) -> p h d", h=XH),
                                          ropex[:, n, 0, t:t + 1, :].to_broadcast([P, XH, XD]), ALU.mult)
                ins.then_inc(sem["cosine"], 1)

            def run(phase, bm, br):
                head = phase in ("second", "body")
                bh = 0 if phase == "first" else bm + 1 if head else None
                ahead = phase in ("first", "body", "next_to_last")
                bk = 0 if phase == "first" else br + 1 if ahead else None
                for step in STEPS[phase]:
                    kind, args = step[0], step[1:]
                    if kind == "proj":
                        t, c = args
                        b = bm if c == 2 else bh
                        n = 2 * c + t
                        width = 512 if c else KV * HD
                        total = rot[:, n % 2, 0, 0:width]
                        pool.wait_ge(sem["rot_prod"], at("rot_prod", b, 3 * n + 2))
                        g.tensor_tensor(total, total, rot[:, n % 2, 1, 0:width], ALU.add).then_inc(sem["rot_sum"], 1)
                        pool.wait_ge(sem["rot_hi"], at("rot_hi", b, n))
                        if c == 0:
                            g.tensor_tensor(ktok[:, t, :, HD:2 * HD], total.rearrange("p (g n) -> p g n", g=KV),
                                            ktok[:, t, :, 0:HD].bitcast(F32), ALU.subtract).then_inc(sem["rot_lo"], 1)
                        else:
                            g.tensor_tensor(qtok[:, t, :, HD:2 * HD], total.rearrange("p (h n) -> p h n", h=8),
                                            qtok[:, t, :, 0:HD].bitcast(F32), ALU.subtract).then_inc(sem["rot_lo"], 1)
                    elif kind == "V":
                        pool.wait_ge(sem["v_new"], at("v_new", bh, 1))
                        pool.wait_ge(sem["O_mm"], at("O_mm", bh - 1, PAIRS - 1))
                        pool.sem_inc(waits_passed, 1)
                        g.tensor_copy(v_sb[:], v_new[:]).then_inc(sem["v_ready"], 1)
                    elif kind == "S":
                        p, q = args
                        if 2 * p + q:
                            normalise(bm, 2 * p + q - 1)
                    elif kind == "T":
                        p, q = args
                        if 2 * p + q == 2 * PAIRS - 2:
                            normalise(bm, 2 * PAIRS - 1)
                    elif kind == "y_stats":
                        ln_rstd(br, LN_Y)
                    elif kind == "ctx_stats":
                        pool.wait_ge(sem["ctx_mv"], at("ctx_mv", bk, 1))
                        pool.sem_inc(waits_passed, 1)
                        g.tensor_scalar(veps[:, LN_CTX, :], mv[:, LN_CTX, :, 1], EPS, None, ALU.add).then_inc(sem["ctx_eps"], 1)
                        pool.wait_ge(sem["ctx_eps"], at("ctx_eps", bk))
                        g.tensor_tensor(rstd[:, LN_CTX, :], veps[:, LN_CTX, :], minus_half[:], ALU.pow).then_inc(sem["ctx_rstd"], 1)
                    elif kind == "y_apply":
                        ln_rstd(br, LN_X1)
                    elif kind == "o_stats":
                        ln_rstd(br, LN_O)
                    elif kind == "y2_stats":
                        ln_rstd(br, LN_Y2)
                    elif kind == "y3_stats":
                        ln_rstd(br, LN_Y3)
                    elif kind == "x1_apply":
                        pool.wait_ge(sem["nx_ready"], at("nx_ready", br, 1))
                        g.tensor_tensor(x1[:], x1[:], brow[:, 3:4, :].to_broadcast([P, TT, D]), ALU.add).then_inc(sem["x1b_ready"], 1)
                    elif kind == "k_turn":
                        pool.wait_ge(sem["kx_raw"], at("kx_raw", bk, 1))
                        cosine_x(0, kx_tok)
                        pool.wait_ge(sem["cosine"], at("cosine", bk, 0))
                        pool.wait_ge(sem["turned"], at("turned", bk, 1))
                        g.tensor_tensor(kx_tok[:], turn[0][:, 0, :, :], turn[0][:, 1, :, :], ALU.add).then_inc(sem["kx_rot"], 1)
                    elif kind == "q_turn":
                        pool.wait_ge(sem["qx_raw"], at("qx_raw", br))
                        cosine_x(1, qx_tok)
                        pool.wait_ge(sem["cosine"], at("cosine", br, 1))
                        pool.wait_ge(sem["turned"], at("turned", br, 3))
                        g.tensor_tensor(qx_tok[:], turn[1][:, 0, :, :], turn[1][:, 1, :, :], ALU.add).then_inc(sem["qx_rot"], 1)
                    elif kind == "KX":
                        t, = args
                        b = bk if t < 2 else br
                        if t == 0:
                            pool.wait_ge(sem["kxT_ready"], at("kxT_ready", b))
                        pool.wait_ge(sem["SX1_mm"], at("SX1_mm", b, 2 * (t - 2) + 1))
                        g.tensor_tensor(kx[:, t % 2, :, :], kxT[:, t // 2:t // 2 + 1, :].to_broadcast([P, 4, L]),
                                        own_head[:, 4 * (t % 2):4 * (t % 2) + 4].unsqueeze(2).to_broadcast([P, 4, L]), ALU.mult)\
                            .then_inc(sem["kx_ready"], 1)

            g.memset(ident[:], 0.0).then_inc(pool_consts, 1)
            g.memset(ident16[:], 0.0).then_inc(pool_consts, 1)
            g.memset(vx[:], 0.0).then_inc(pool_consts, 1)
            g.memset(px1[:], 0.0).then_inc(pool_consts, 1)
            g.memset(minus_half[:], -0.5).then_inc(pool_consts, 1)
            g.memset(ones, 1.0).then_inc(pool_consts, 1)
            pool.wait_ge(pool_consts, 6)
            for m in (ident, ident16):
                g.affine_select(out=m[:], in_=m[:], compare_op=ALU.not_equal, fill=1.0, base=0,
                                pattern=[[-1, P]], channel_multiplier=1).then_inc(pool_consts, 1)
            pool.wait_ge(pre_dve, PRE_DVE)
            run("first", None, None)
            run("second", 0, None)
            with pool.Fori(0, B - 2) as j:
                run("body", j + 1, j)
            run("next_to_last", B - 1, B - 2)
            run("last", None, B - 1)


def rope_table(n, dim, first, interleaved):
    inv = (np.float32(1.0) / np.power(np.float32(10000.0), np.arange(0, dim, 2, dtype=np.float32) / np.float32(dim))).astype(np.float32)
    freqs = (np.arange(first, first + n, dtype=np.float32)[:, None] * inv[None, :]).astype(np.float32)
    emb = np.repeat(freqs, 2, axis=-1) if interleaved else np.concatenate([freqs, freqs], axis=-1)
    emb = emb.astype(np.float64).T
    return np.cos(emb), np.sin(emb)


def by_token(table):
    return table.reshape(TT, P, -1).transpose(1, 0, 2).reshape(P, -1)


def constants():
    f = lambda x: np.ascontiguousarray(x, dtype=np.float32)
    cos, sin = rope_table(L, HD, 0, False)
    sgn = np.where(np.arange(HD) < HD // 2, -1.0, 1.0)
    rope = np.concatenate([by_token(cos.T), by_token(sin.T * sgn)], axis=1)
    slopes = np.array([(2.0 ** -0.5) ** (i + 1) for i in range(2)], dtype=np.float32)
    rel = (np.arange(L)[None, :] - np.arange(P)[:, None]).astype(np.float32)
    alibi = (slopes[:, None, None] * rel[None]).transpose(1, 0, 2).reshape(P, -1)
    sg = np.where(np.arange(XD) % 2 == 0, -1.0, 1.0)
    ropex = []
    for first, scale in ((WIN, 1.0), (0, 0.25)):
        cx, sx = rope_table(L, XD, first, True)
        ropex += [by_token(cx.T * scale), by_token(sx.T * sg * scale)]
    q, k = np.arange(L)[:, None], np.arange(L)[None, :]
    bad = ((k > q) | (k // WIN < q // WIN - 1)).astype(np.float32)
    own_head = np.repeat(np.eye(8), XD, axis=0)
    return dict(own_head=f(own_head), rope=f(rope), alibi=f(alibi), ropex=f(np.concatenate(ropex, axis=1)),
                pen0=f(bad[0:P, 0:P]), pen1=f(bad[P:, WIN:]))


def kernel(**inputs):
    import concourse.bacc as bacc
    from concourse.bass_utils import run_bass_kernel_spmd as launch

    t = {k: np.asarray(v) for k, v in inputs.items()}
    x = t["x"].reshape(B * L, D)
    xa = lambda n: t["L0_xattn_" + n]
    gb = np.stack([xa(f"ln_{n}_{c}").reshape(D) for n in "qkvo" for c in "wb"])
    arrays = dict(
        x=x, xT=x.T, ctx=t["ctx_1024"].reshape(B * L, D), cell=t["itok_Bx1xSx1_0_63"].reshape(B * L),
        wqkv=np.concatenate([t["L0_attn_Wk"], t["L0_attn_Wv"], t["L0_attn_Wq"]], axis=1), wo=t["L0_attn_Wo"],
        wqx=xa("w_q").T, wkvx=np.concatenate([xa("w_k").T, xa("w_v").T], axis=1), wox=xa("w_o").T,
        gb=gb.reshape(8, KT, P).transpose(2, 0, 1).reshape(P, 8 * KT),
        b_q=xa("b_q"), b_k=xa("b_k"), b_v=xa("b_v"), b_o=xa("b_o"),
        wg=t["L0_ffn_w_gate"].T, wu=t["L0_ffn_w_up"].T, wd=t["L0_ffn_w_down"].T,
        **constants(),
    )
    arrays = {k: np.ascontiguousarray(v) for k, v in arrays.items()}
    nc = bacc.Bacc("TRN2", target_bir_lowering=False, num_devices=1)
    aps = {k: nc.dram_tensor(f"in_{k}", v.shape, mybir.dt.from_np(v.dtype), kind="ExternalInput").ap() for k, v in arrays.items()}
    out = nc.dram_tensor("out_y", (B * L, D), F32, kind="ExternalOutput").ap()
    build(nc, aps, out)
    r = launch(nc, [{f"in_{k}": v for k, v in arrays.items()}], core_ids=[0])
    return r.results[0]["out_y"].reshape(B, L, D)
```

```python
from contextlib import ExitStack

import numpy as np

import concourse.bass as bass
from concourse import mybir

ALU = mybir.AluOpType
ACT = mybir.ActivationFunctionType
F32 = mybir.dt.float32
BF16 = mybir.dt.bfloat16
F32R = mybir.dt.float32r
I32 = mybir.dt.int32
AX_X = mybir.AxisListType.X

P = 128
B, L, D = 32, 256, 256
TT = L // P
KT = D // P
H, KV, HD = 16, 4, 64
PAIRS = H // 2
XH, XD = 16, 16
WIN = 64
XT = 4
K1 = L - WIN
INNER = 1024
IC = INNER // P
MAGIC = 12582912.0
BIG = 1.0e30
EPS = 1e-5
CREDIT = 2

COUNT = dict(
    xT_loaded=16, xtok_loaded=16, ctx_loaded=16, cell_loaded=32, stored=16,
    proj_mm=6, kT_mm=4, qT_mm=8, S_mm=16, T_mm=16, O_mm=8, W_mm=1,
    x_hi=1, x_lo=1, v_new=2, v_ready=1, rot_prod=18, rot_sum=6, rot_hi=6, rot_lo=6, k_ready=4, q_ready=8,
    s_neg=32, p_exp=32, p_recip=16, p_norm=16, pT_ready=16, oT_ready=8, y_ready=1,
    ln_stats=8, ln_mv=8, ln_eps=4, ln_rstd=4, ctx_stats=2, ctx_mv=2, ctx_eps=1, ctx_rstd=1,
    y3_stats=2, y3_mv=2, y3_eps=1, y3_rstd=1, x1_ready=2, x1b_ready=1, nc_ready=2, nx_ready=2, no_ready=2,
    x2_ready=2, out_ready=2,
    C_mm=1, NX_mm=1, KV_mm=2, QX_mm=1, KXT_mm=1, QXT_mm=1, SX0_mm=4, SX1_mm=8, TX0_mm=4, TX1_mm=8,
    OX_mm=4, BX_mm=2, NO_mm=1, PO_mm=1,
    cellq_ready=1, pen_ready=2, mask_ready=2, cT_ready=1, nT_ready=1, kx_raw=2, vx_ready=2, qx_raw=1,
    turned=4, cosine=2, kx_rot=1, qx_rot=1, kxT_ready=1, qxT_ready=1, kx_ready=4,
    sx0_neg=16, sx1_neg=16, px0_exp=16, px1_exp=16, pTx0_ready=4, pTx1_ready=8, ox_ready=4,
    sx_recip=2, o_ready=2, noT_ready=1, y2_ready=1,
    XQ_mm=1, G_mm=4, U_mm=4, HT_mm=2, D_mm=1, quant_x=6, xq_shift=2, xq_ready=1, xs_tanh=1, xs_half=1,
    xqT_ready=1, tanh_ready=4, gate_ready=4, h_ready=4, quant_h=10, hq_shift=2, hq_ready=2, hqT_ready=2, y3_ready=2,
)
LN_Y, LN_X1, LN_O, LN_Y2, LN_Y3, LN_CTX = range(6)

BANKS = dict(S=(0, 1), T=2, proj=3, kT=4, qT=4, O=4, W=4, SX=5, G=5, TX=6, U=6, chain=7)


BODY = [
    ('S', 0, 0), ('quant_x',), ('S', 0, 1), ('R', 0, 0), ('W',), ('qT', 2), ('y_stats',), ('S', 1, 0), ('XQ',),
    ('R', 0, 1), ('G', 0, 0), ('y_apply',), ('U', 0, 0), ('T', 0, 0), ('S', 1, 1), ('R', 1, 0), ('S', 2, 0),
    ('x1_apply',), ('G', 0, 1), ('qT', 3), ('T', 0, 1), ('proj', 0, 2), ('NX',), ('U', 0, 1), ('R', 1, 1),
    ('proj', 1, 2), ('T', 1, 0), ('quant_h', 0), ('O', 0), ('QX',), ('G', 1, 0), ('S', 2, 1), ('q_turn',),
    ('T', 1, 1), ('qT', 4), ('U', 1, 0), ('R', 2, 0), ('HT', 0), ('G', 1, 1), ('R', 2, 1), ('S', 3, 0), ('QXT',),
    ('U', 1, 1), ('R', 3, 0), ('T', 2, 0), ('O', 1), ('S', 3, 1), ('SX0', 0), ('T', 2, 1), ('R', 3, 1), ('qT', 5),
    ('quant_h', 1), ('T', 3, 0), ('SX1', 0, 0), ('T', 3, 1), ('TX0', 0), ('O', 2), ('SX1', 0, 1), ('HT', 1),
    ('TX1', 0, 0), ('S', 4, 0), ('SX0', 1), ('KX', 2), ('R', 4, 0), ('S', 4, 1), ('S', 5, 0), ('qT', 6),
    ('SX1', 1, 0), ('ctx_stats',), ('D',), ('TX1', 0, 1), ('O', 3), ('SX1', 1, 1), ('R', 4, 1), ('TX0', 1), ('X',),
    ('T', 4, 0), ('OX', 0), ('TX1', 1, 0), ('S', 5, 1), ('SX0', 2), ('KX', 3), ('R', 5, 0), ('T', 4, 1),
    ('TX1', 1, 1), ('S', 6, 0), ('SX1', 2, 0), ('proj', 0, 0), ('T', 5, 0), ('R', 5, 1), ('TX0', 2), ('S', 6, 1),
    ('SX1', 2, 1), ('y3_stats',), ('qT', 7), ('TX1', 2, 0), ('proj', 1, 0), ('SX0', 3), ('T', 5, 1), ('OX', 1),
    ('S', 7, 0), ('TX1', 2, 1), ('SX1', 3, 0), ('proj', 0, 1), ('R', 6, 0), ('SX1', 3, 1), ('TX0', 3), ('O', 4),
    ('OX', 2), ('TX1', 3, 0), ('S', 7, 1), ('R', 6, 1), ('TX1', 3, 1), ('ctx_apply',), ('mask',), ('T', 6, 0),
    ('O', 5), ('OX', 3), ('BX', 0), ('R', 7, 0), ('kT', 0), ('BX', 1), ('o_stats',), ('kT', 1), ('T', 6, 1), ('C',),
    ('R', 7, 1), ('o_apply',), ('O', 6), ('T', 7, 0), ('NO',), ('kT', 2), ('PO',), ('proj', 1, 1), ('KV', 0),
    ('kT', 3), ('T', 7, 1), ('y3_apply',), ('KV', 1), ('k_turn',), ('y2_stats',), ('qT', 0), ('y2_apply',), ('O', 7),
    ('qT', 1), ('KXT',), ('KX', 0), ('KX', 1), ('V',),
]

SELF = ("X", "proj", "kT", "qT", "S", "R", "T", "O", "V")
KEYS = ("ctx_stats", "ctx_apply", "C", "KV", "k_turn", "mask", "KXT")
FEED = ("quant_x", "XQ", "quant_h", "G", "U", "HT", "D", "y3_stats", "y3_apply")


def of_self(step):
    return step[0] in SELF


def of_head(step):
    return step[0] in ("X", "kT", "V") or (step[0] == "proj" and step[2] < 2) or (step[0] == "qT" and step[1] < 2)


def of_keys(step):
    return step[0] in KEYS or (step[0] == "KX" and step[1] < 2)


def of_feed(step):
    return step[0] in FEED


STEPS = dict(
    first=[x for x in BODY if of_head(x)],
    second=[x for x in BODY if of_self(x) or of_keys(x)],
    third=[x for x in BODY if not of_feed(x)],
    body=BODY,
    next_to_last=[x for x in BODY if not of_head(x)],
    last=[x for x in BODY if not of_self(x) and not of_keys(x)],
    final=[x for x in BODY if of_feed(x)],
)


def at(name, batch, k=0):
    return (batch + CREDIT) * COUNT[name] + (k + 1)


def landed(name, batch):
    return (batch + CREDIT + 1) * COUNT[name]


def build(nc, a, out):
    with ExitStack() as ctx:
        def sb(name, shape, dt=F32):
            return ctx.enter_context(nc.sbuf_tensor(name, shape, dt))

        sem = {name: ctx.enter_context(nc.semaphore(name)) for name in COUNT}
        proj_loaded = ctx.enter_context(nc.semaphore("proj_loaded"))
        weights_loaded = ctx.enter_context(nc.semaphore("weights_loaded"))
        pool_consts = ctx.enter_context(nc.semaphore("pool_consts"))
        pre_dve = ctx.enter_context(nc.semaphore("pre_dve"))
        waits_passed = ctx.enter_context(nc.semaphore("waits_passed"))
        pre_pe = ctx.enter_context(nc.semaphore("pre_pe"))

        psum = [ctx.enter_context(nc.psum_tensor(f"bank{i}", [P, 512], F32)) for i in range(8)]

        QKV = (2 * KV + H) * HD
        w_hi = sb("w_hi", [P, KT, QKV], F32R)
        w_lo = sb("w_lo", [P, KT, QKV], F32R)
        wo = sb("wo", [P, PAIRS, D])
        rope = sb("rope", [P, 2, TT, HD])
        alibi = sb("alibi", [P, 2, L])
        wqx = sb("wqx", [P, KT, D])
        wkvx = sb("wkvx", [P, KT, 2 * D])
        wox = sb("wox", [P, KT, D])
        ropex = sb("ropex", [P, 2, 2, TT, XD])
        pen0 = sb("pen0", [P, P])
        pen1 = sb("pen1", [P, K1])
        gb = sb("gb", [P, 8, KT])
        brow = sb("brow", [P, 4, D])
        wg16 = sb("wg16", [P, KT, INNER], BF16)
        wu16 = sb("wu16", [P, KT, INNER], BF16)
        wd16 = sb("wd16", [P, IC, D], BF16)
        ident = sb("ident", [P, P])
        ident16 = sb("ident16", [P, P], BF16)
        wsum = sb("wsum", [P, 3])
        wmean = sb("wmean", [P, 3])
        wrec = sb("wrec", [P, 3])
        wk1 = sb("wk1", [P, 3])

        xT = sb("xT", [P, KT, L])
        x_hi = sb("x_hi", [P, KT, L], F32R)
        x_lo = sb("x_lo", [P, KT, L], F32R)
        xtok = sb("xtok", [P, TT, D])
        ctxt = sb("ctxt", [P, TT, D])
        cellk = sb("cellk", [P, L], I32)
        cellq = sb("cellq", [P, TT], I32)
        cellqf = sb("cellqf", [P, TT])
        v_new = sb("v_new", [P, TT, KV * HD])
        v_sb = sb("v_sb", [P, TT, KV * HD])
        rot = sb("rot", [P, 3, 512])
        ktok = sb("ktok", [P, TT, KV, 3 * HD], F32R)
        qtok = sb("qtok", [P, TT, 8, 2 * HD], F32R)
        kk = sb("kk", [P, 2, KV, L], F32R)
        qq = sb("qq", [P, 3, 2, L], F32R)
        prob = sb("prob", [P, 4, 2, L])
        nmax = sb("nmax", [P, 2 * H])
        psums = sb("psums", [P, 2 * H])
        precs = sb("precs", [P, 2 * H])
        pT = sb("pT", [P, 2, 2, TT, L])
        oT = sb("oT", [P, PAIRS, L])
        bn = sb("bn", [P, 6, TT, 6])
        mv = sb("mv", [P, 6, TT, 2])
        own_head = sb("own_head", [P, 8])
        veps = sb("veps", [P, 6, TT])
        rstd = sb("rstd", [P, 6, TT])
        minus_half = sb("minus_half", [P, TT])
        x1 = sb("x1", [P, TT, D])
        y = x1
        nx = sb("nx", [P, TT, D])
        nT = sb("nT", [P, KT, L])
        ncx = ctxt
        cT = sb("cT", [P, KT, L])
        mask0 = sb("mask0", [P, P])
        mask1 = sb("mask1", [P, K1])
        pm0, pm1 = mask0, mask1
        kxT = sb("kxT", [P, 2, L])
        kx = sb("kx", [P, 2, 4, L])
        vx = sb("vx", [P, TT, XH, 32])
        qx = cT
        px0 = sb("px0", [P, 2, 4, P])
        px1 = sb("px1", [P, 3, 2, L])
        nmx = sb("nmx", [P, TT, XH])
        sumx = sb("sumx", [P, TT, XH])
        recx = sb("recx", [P, TT, XH])
        pTx = sb("pTx", [P, 2, 4, 3, P])
        ox = sb("ox", [P, XT, L])
        n_o, noT = nx, nT
        y2 = sb("y2", [P, TT, D])
        o_tok = y2
        x2 = sb("x2", [P, TT, D])
        amx = sb("amx", [P, TT])
        ax = sb("ax", [P, 7, TT])
        xqT = sb("xqT", [P, KT, L], BF16)
        hh = sb("hh", [P, TT, INNER])
        xshift = hh[:, 0, 0:TT * D].rearrange("p (t n) -> p t n", t=TT)
        hs = sb("hs", [P, 6, TT])
        hq = sb("hq", [P, INNER], BF16)
        xq = hq[:, 0:TT * D].rearrange("p (t n) -> p t n", t=TT)
        hqT = sb("hqT", [P, TT, IC, P], BF16)
        y3 = sb("y3", [P, TT, D])
        kx_tok, qx_tok = nx, y2
        turn = [pTx[:].rearrange("p s h c n -> p (s h c n)")[:, n * 4 * D:(n + 1) * 4 * D].rearrange("p (c t n) -> p c t n", c=2, t=TT)
                for n in range(2)]

        stage = [prob[:].rearrange("p s c n -> p (s c n)"), oT[:].rearrange("p h n -> p (h n)"),
                 pTx[:, 0:2, :, :, :].rearrange("p t h c n -> p (t h c n)")[:, 0:2048]]
        raw_w = [hh[:].rearrange("p t n -> p (t n)")[:, 0:QKV], pT[:].rearrange("p s c k n -> p (s c k n)")[:, 0:QKV]]
        ones = qx[:, 0, 0:P]
        bwide = px0[:].rearrange("p c h n -> p (c h n)").rearrange("p (c k n) -> p c k n", c=4, k=KT)

        LN = [y, x1, o_tok, y2]

        first_loads = [
            (raw_w[0], a["wqkv"][0:P, :]), (raw_w[1], a["wqkv"][P:2 * P, :]),
            (rope[:].rearrange("p c t n -> p (c t n)"), a["rope"]),
        ]
        flat_loads = [
            (alibi[:].rearrange("p h n -> p (h n)"), a["alibi"]),
            (stage[0].rearrange("p (k n) -> p k n", k=KT), a["wg"].rearrange("(k p) n -> p k n", p=P)),
            (stage[1].rearrange("p (k n) -> p k n", k=KT), a["wu"].rearrange("(k p) n -> p k n", p=P)),
            (stage[2].rearrange("p (k n) -> p k n", k=IC), a["wd"].rearrange("(k p) n -> p k n", p=P)),
            (wo[:], a["wo"].rearrange("(k p) n -> p k n", p=P)),
            (wqx[:], a["wqx"].rearrange("(k p) n -> p k n", p=P)),
            (wkvx[:], a["wkvx"].rearrange("(k p) n -> p k n", p=P)),
            (wox[:], a["wox"].rearrange("(k p) n -> p k n", p=P)),
            (ropex[:].rearrange("p a c t n -> p (a c t n)"), a["ropex"]),
            (own_head[:], a["own_head"]), (pen0[:], a["pen0"]), (pen1[:], a["pen1"]),
            (gb[:].rearrange("p c k -> p (c k)"), a["gb"]),
        ] + [(brow[:, n, :], a["b_" + c].rearrange("(a n) -> a n", a=1).to_broadcast([P, D])) for n, c in enumerate("qkvo")]
        N_LOADS = 16 * len(flat_loads)

        xT_dram = a["xT"].rearrange("(k p) t -> p k t", p=P)
        x_dram = a["x"].rearrange("(b t p) d -> b p t d", t=TT, p=P)
        ctx_dram = a["ctx"].rearrange("(b t p) d -> b p t d", t=TT, p=P)
        cell_cols = a["cell"].rearrange("(b t p) -> b p t", t=TT, p=P)
        cell_rows = a["cell"].rearrange("(b t) -> b t", t=L)
        out_dram = out.rearrange("(b t p) d -> b p t d", t=TT, p=P)

        PRE_DVE = 35
        POOL_CONSTS = 8

        block = ctx.enter_context(nc.Block())

        @block.sync
        def _(sp):
            for name, n in COUNT.items():
                sp.sem_inc(sem[name], CREDIT * n)

            def one(ap, b):
                return ap[bass.ds(b, 1)]

            def load_ctx(b):
                sp.wait_ge(sem["C_mm"], at("C_mm", b - 1))
                sp.dma_start(ctxt[:], one(ctx_dram, b).rearrange("a p t d -> (a p) t d")).then_inc(sem["ctx_loaded"], 16)
                sp.wait_ge(sem["pen_ready"], at("pen_ready", b - 1, 1))
                sp.dma_start(cellq[:], one(cell_cols, b).rearrange("a p t -> (a p) t"),
                             allow_slow_non_contiguous=True).then_inc(sem["cell_loaded"], 16)
                sp.dma_start(cellk[:], one(cell_rows, b).to_broadcast([P, L])).then_inc(sem["cell_loaded"], 16)

            def load_xT(b):
                sp.wait_ge(sem["x_hi"], at("x_hi", b - 1))
                sp.wait_ge(sem["x_lo"], at("x_lo", b - 1))
                sp.dma_start(xT[:], xT_dram[:, :, bass.ds(b * L, L)]).then_inc(sem["xT_loaded"], 16)

            def load_xtok(b):
                sp.wait_ge(sem["y_ready"], at("y_ready", b - 1))
                sp.dma_start(xtok[:], one(x_dram, b).rearrange("a p t d -> (a p) t d")).then_inc(sem["xtok_loaded"], 16)

            def store(b):
                sp.wait_ge(sem["out_ready"], at("out_ready", b, 1))
                sp.dma_start(one(out_dram, b).rearrange("a p t d -> (a p) t d"), y3[:]).then_inc(sem["stored"], 16)

            load_xT(0)
            for dst, src in first_loads:
                sp.dma_start(dst, src).then_inc(proj_loaded, 16)
            for dst, src in flat_loads:
                sp.dma_start(dst, src).then_inc(weights_loaded, 16)
            load_xtok(0)
            load_ctx(0)
            load_xT(1)
            load_ctx(1)
            load_xT(2)
            load_xtok(1)
            load_ctx(2)
            load_xT(3)
            with sp.Fori(0, B - 4) as j:
                load_xtok(j + 2)
                store(j)
                load_ctx(j + 3)
                load_xT(j + 4)
            load_xtok(B - 2)
            store(B - 4)
            load_ctx(B - 1)
            load_xtok(B - 1)
            store(B - 3)
            store(B - 2)
            store(B - 1)
            sp.wait_ge(sem["stored"], landed("stored", B - 1))

        @block.tensor
        def _(pe):
            mm = nc.tensor.matmul

            def transposes(bank, blocks):
                for n, src in enumerate(blocks):
                    last = nc.tensor.transpose(bank[:, n * P:(n + 1) * P], src, ident[:])
                return last

            def transposes_r(bank, blocks):
                for n, src in enumerate(blocks):
                    last = nc.tensor.transpose(bank[:, n * P:(n + 1) * P], src.bitcast(F32), ident[:])
                return last

            def transposes16(bank, blocks):
                for n, src in enumerate(blocks):
                    last = nc.tensor.transpose(bank[:].bitcast(BF16)[:, n * P:(n + 1) * P], src, ident16[:])
                return last

            def run(phase, bm, br):
                head = phase in ("second", "third", "body")
                bh = 0 if phase == "first" else bm + 1 if head else None
                ahead = phase in ("second", "third", "body", "next_to_last")
                bk = br + 1 if ahead else None
                bf = None if phase == "first" else br - 1
                for step in STEPS[phase]:
                    kind, args = step[0], step[1:]
                    if kind == "proj":
                        t, c = args
                        b = bm if c == 2 else bh
                        if c < 2 and t == 0:
                            pe.wait_ge(sem["x_hi"], at("x_hi", b))
                            pe.wait_ge(sem["x_lo"], at("x_lo", b))
                        if (t, c) == (0, 0):
                            pe.wait_ge(sem["rot_prod"], at("rot_prod", b - 1, 17))
                        else:
                            pe.wait_ge(sem["rot_prod"], at("rot_prod", b, 3 * (2 * c + t) - 1))
                        if (t, c) in ((1, 0), (0, 1)):
                            pe.wait_ge(sem["v_new"], at("v_new", b, 2 * c + t - 1))
                        parts = ((x_hi, w_hi), (x_lo, w_hi), (x_hi, w_lo))
                        for i in range(KT * 3):
                            k, (xs, ws) = i // 3, parts[i % 3]
                            last = mm(psum[BANKS["proj"]][:], xs[:, k, t * P:(t + 1) * P], ws[:, k, c * 512:(c + 1) * 512],
                                      start=i == 0, stop=i == KT * 3 - 1)
                        last.then_inc(sem["proj_mm"], 1)
                    elif kind == "kT":
                        i, = args
                        t, h = i % 2, i // 2
                        pe.wait_ge(sem["rot_lo"], at("rot_lo", bh, t))
                        if i == 0:
                            pe.wait_ge(sem["oT_ready"], at("oT_ready", bh - 1, PAIRS - 3))
                        elif i == 1:
                            pe.wait_ge(sem["k_ready"], at("k_ready", bh, 0))
                        elif i == 2:
                            pe.wait_ge(sem["k_ready"], at("k_ready", bh, 1))
                            pe.wait_ge(sem["oT_ready"], at("oT_ready", bh - 1, PAIRS - 2))
                        else:
                            pe.wait_ge(sem["k_ready"], at("k_ready", bh, 2))
                        transposes_r(psum[BANKS["kT"]], [ktok[:, t, g, c * HD:c * HD + P] for g in (2 * h, 2 * h + 1) for c in range(2)])\
                            .then_inc(sem["kT_mm"], 1)
                    elif kind == "qT":
                        p, = args
                        b = bh if p < 2 else bm
                        if p % 4 == 0:
                            pe.wait_ge(sem["rot_lo"], at("rot_lo", b, 3 if p < 4 else 5))
                        if p == 0:
                            pe.wait_ge(sem["k_ready"], at("k_ready", b, 3))
                        elif p == 1:
                            pe.wait_ge(sem["q_ready"], at("q_ready", b, 0))
                            pe.wait_ge(sem["oT_ready"], at("oT_ready", b - 1, PAIRS - 1))
                        elif p == 2:
                            pe.wait_ge(sem["y_ready"], at("y_ready", b - 1))
                            pe.wait_ge(sem["q_ready"], at("q_ready", b, 1))
                        elif p == 3:
                            pe.wait_ge(sem["q_ready"], at("q_ready", b, 2))
                        else:
                            pe.wait_ge(sem["oT_ready"], at("oT_ready", b, p - 4))
                        transposes_r(psum[BANKS["qT"]], [qtok[:, t, 2 * (p % 4) + c, :] for c in range(2) for t in range(TT)])\
                            .then_inc(sem["qT_mm"], 1)
                    elif kind == "S":
                        p, q = args
                        n = 2 * p + q
                        if q == 0:
                            pe.wait_ge(sem["q_ready"], at("q_ready", bm, p))
                        if n == 0:
                            pe.wait_ge(sem["k_ready"], at("k_ready", bm, 3))
                        pe.wait_ge(sem["s_neg"], at("s_neg", bm, 2 * n - 3))
                        for c in range(2):
                            for i in range(2):
                                last = mm(psum[BANKS["S"][n % 2]][:, c * L:(c + 1) * L], qq[:, p % 3, c, q * P:(q + 1) * P],
                                          kk[:, i, p // 2, :], start=i == 0, stop=i == 1)
                        last.then_inc(sem["S_mm"], 1)
                    elif kind == "T":
                        p, q = args
                        n = 2 * p + q
                        pe.wait_ge(sem["p_norm"], at("p_norm", bm, n))
                        pe.wait_ge(sem["pT_ready"], at("pT_ready", bm, n - 1))
                        transposes(psum[BANKS["T"]], [prob[:, n % 4, c, k * P:(k + 1) * P] for c in range(2) for k in range(TT)])\
                            .then_inc(sem["T_mm"], 1)
                    elif kind == "O":
                        p, = args
                        if p == 0:
                            pe.wait_ge(sem["v_ready"], at("v_ready", bm))
                        pe.wait_ge(sem["pT_ready"], at("pT_ready", bm, 2 * p + 1))
                        if p <= PAIRS - 4:
                            pe.wait_ge(sem["q_ready"], at("q_ready", bm, p + 3))
                        elif head and p == PAIRS - 2:
                            pe.wait_ge(sem["k_ready"], at("k_ready", bh, 1))
                        elif head and p == PAIRS - 1:
                            pe.wait_ge(sem["q_ready"], at("q_ready", bh, 0))
                        else:
                            pe.wait_ge(sem["oT_ready"], at("oT_ready", bm, p - 1))
                        for k in range(TT):
                            for c in range(2):
                                last = mm(psum[BANKS["O"]][c * HD:(c + 1) * HD, 0:L], v_sb[:, k, (p // 2) * HD:(p // 2 + 1) * HD],
                                          pT[:, p % 2, c, k, :], start=k == 0, stop=k == TT - 1)
                        last.then_inc(sem["O_mm"], 1)
                    elif kind == "W":
                        pe.wait_ge(sem["oT_ready"], at("oT_ready", br, PAIRS - 1))
                        if phase != "last":
                            pe.wait_ge(sem["q_ready"], at("q_ready", bm, 1))
                        for t in range(TT):
                            for k in range(PAIRS):
                                last = mm(psum[BANKS["W"]][:, t * D:(t + 1) * D], oT[:, k, t * P:(t + 1) * P], wo[:, k, :],
                                          start=k == 0, stop=k == PAIRS - 1)
                        last.then_inc(sem["W_mm"], 1)
                    elif kind == "C":
                        pe.wait_ge(sem["nc_ready"], at("nc_ready", bk, 1))
                        pe.wait_ge(sem["o_ready"], at("o_ready", bk - 1, 1))
                        transposes(psum[7], [ncx[:, t, k * P:(k + 1) * P] for k in range(KT) for t in range(TT)]).then_inc(sem["C_mm"], 1)
                    elif kind == "NX":
                        pe.wait_ge(sem["nx_ready"], at("nx_ready", br, 1))
                        if phase == "third":
                            pe.wait_ge(sem["kxT_ready"], at("kxT_ready", br))
                        else:
                            pe.wait_ge(sem["xqT_ready"], at("xqT_ready", br - 1))
                        transposes(psum[7], [nx[:, t, k * P:(k + 1) * P] for k in range(KT) for t in range(TT)]).then_inc(sem["NX_mm"], 1)
                    elif kind == "NO":
                        pe.wait_ge(sem["no_ready"], at("no_ready", br, 1))
                        if ahead:
                            pe.wait_ge(sem["cT_ready"], at("cT_ready", bk))
                        transposes(psum[7], [n_o[:, t, k * P:(k + 1) * P] for k in range(KT) for t in range(TT)]).then_inc(sem["NO_mm"], 1)
                    elif kind == "KV":
                        t, = args
                        if t == 0:
                            pe.wait_ge(sem["cT_ready"], at("cT_ready", bk))
                            pe.wait_ge(sem["y2_ready"], at("y2_ready", bk - 1))
                        else:
                            pe.wait_ge(sem["kx_raw"], at("kx_raw", bk, 0))
                            pe.wait_ge(sem["vx_ready"], at("vx_ready", bk, 0))
                        for k in range(KT):
                            last = mm(psum[7][:], cT[:, k, t * P:(t + 1) * P], wkvx[:, k, :], start=k == 0, stop=k == KT - 1)
                        last.then_inc(sem["KV_mm"], 1)
                    elif kind == "QX":
                        pe.wait_ge(sem["nT_ready"], at("nT_ready", br))
                        for t in range(TT):
                            for k in range(KT):
                                last = mm(psum[7][:, t * D:(t + 1) * D], nT[:, k, t * P:(t + 1) * P], wqx[:, k, :],
                                          start=k == 0, stop=k == KT - 1)
                        last.then_inc(sem["QX_mm"], 1)
                    elif kind == "KXT":
                        pe.wait_ge(sem["kx_rot"], at("kx_rot", bk))
                        pe.wait_ge(sem["kx_raw"], at("kx_raw", bk, 1))
                        pe.wait_ge(sem["vx_ready"], at("vx_ready", bk, 1))
                        transposes(psum[7], [kx_tok[:, t, k * P:(k + 1) * P] for k in range(KT) for t in range(TT)])\
                            .then_inc(sem["KXT_mm"], 1)
                    elif kind == "QXT":
                        pe.wait_ge(sem["qx_rot"], at("qx_rot", br))
                        pe.wait_ge(sem["hqT_ready"], at("hqT_ready", br - 1, 0))
                        transposes(psum[7], [qx_tok[:, t, k * P:(k + 1) * P] for k in range(KT) for t in range(TT)])\
                            .then_inc(sem["QXT_mm"], 1)
                    elif kind == "SX0":
                        t, = args
                        pe.wait_ge(sem["kx_ready"], at("kx_ready", br, t))
                        if t == 0:
                            pe.wait_ge(sem["qxT_ready"], at("qxT_ready", br))
                            pe.wait_ge(sem["gate_ready"], at("gate_ready", br - 1, 3))
                        else:
                            pe.wait_ge(sem["sx1_neg"], at("sx1_neg", br, 4 * t - 1))
                        mm(psum[BANKS["SX"]][:].rearrange("p (h n) -> p h n", h=4), qx[:, t // 2, 0:P], kx[:, t % 2, :, 0:P],
                           start=True, stop=True).then_inc(sem["SX0_mm"], 1)
                    elif kind == "SX1":
                        t, h = args
                        if h == 0:
                            pe.wait_ge(sem["sx0_neg"], at("sx0_neg", br, 4 * t + 3))
                        else:
                            pe.wait_ge(sem["sx1_neg"], at("sx1_neg", br, 4 * t + 1))
                        mm(psum[BANKS["SX"]][:, 0:2 * K1].rearrange("p (h n) -> p h n", h=2), qx[:, t // 2, P:2 * P],
                           kx[:, t % 2, 2 * h:2 * h + 2, WIN:L], start=True, stop=True).then_inc(sem["SX1_mm"], 1)
                    elif kind == "TX0":
                        t, = args
                        pe.wait_ge(sem["px0_exp"], at("px0_exp", br, 4 * t + 3))
                        if t == 0:
                            pe.wait_ge(sem["h_ready"], at("h_ready", br - 1, 3))
                        else:
                            pe.wait_ge(sem["pTx1_ready"], at("pTx1_ready", br, 2 * t - 1))
                        transposes(psum[BANKS["TX"]], [px0[:, t % 2, h, :] for h in range(4)]).then_inc(sem["TX0_mm"], 1)
                    elif kind == "TX1":
                        t, h = args
                        n = 2 * t + h
                        pe.wait_ge(sem["px1_exp"], at("px1_exp", br, 2 * n + 1))
                        if h == 0:
                            pe.wait_ge(sem["pTx0_ready"], at("pTx0_ready", br, t))
                        else:
                            pe.wait_ge(sem["pTx1_ready"], at("pTx1_ready", br, n - 1))
                        transposes(psum[BANKS["TX"]], [px1[:, n % 3, c, k * P:(k + 1) * P] for c in range(2) for k in range(TT)])\
                            .then_inc(sem["TX1_mm"], 1)
                    elif kind == "OX":
                        t, = args
                        pe.wait_ge(sem["pTx1_ready"], at("pTx1_ready", br, 2 * t + 1))
                        if t:
                            pe.wait_ge(sem["ox_ready"], at("ox_ready", br, t - 1))
                        else:
                            pe.wait_ge(sem["vx_ready"], at("vx_ready", br, 1))
                            pe.wait_ge(sem["y3_ready"], at("y3_ready", br - 1, 1))
                        for blk, kt, first, last_ in ((0, 0, True, True), (1, 0, True, False), (2, 1, False, True)):
                            col = P if blk else 0
                            for h in range(4):
                                last = mm(psum[7][32 * h:32 * h + 32, col:col + P], vx[:, kt, 4 * t + h, :],
                                          pTx[:, t % 2, h, blk, :], start=first, stop=last_)
                        last.then_inc(sem["OX_mm"], 1)
                    elif kind == "BX":
                        q, = args
                        if q == 0:
                            pe.wait_ge(sem["ox_ready"], at("ox_ready", br, 3))
                        else:
                            pe.wait_ge(sem["o_ready"], at("o_ready", br, 0))
                        transposes(psum[7], [ox[:, t, q * P:(q + 1) * P] for t in range(XT)]).then_inc(sem["BX_mm"], 1)
                    elif kind == "PO":
                        pe.wait_ge(sem["noT_ready"], at("noT_ready", br))
                        for t in range(TT):
                            for k in range(KT):
                                last = mm(psum[7][:, t * D:(t + 1) * D], noT[:, k, t * P:(t + 1) * P], wox[:, k, :],
                                          start=k == 0, stop=k == KT - 1)
                        last.then_inc(sem["PO_mm"], 1)
                    elif kind == "XQ":
                        pe.wait_ge(sem["xq_ready"], at("xq_ready", bf))
                        if phase != "final":
                            pe.wait_ge(sem["kxT_ready"], at("kxT_ready", br))
                        transposes16(psum[7], [xq[:, t, k * P:(k + 1) * P] for k in range(KT) for t in range(TT)])\
                            .then_inc(sem["XQ_mm"], 1)
                    elif kind == "G":
                        t, c = args
                        if (t, c) == (0, 0):
                            pe.wait_ge(sem["xqT_ready"], at("xqT_ready", bf))
                            pe.wait_ge(sem["sx1_neg"], at("sx1_neg", bf, 15))
                        else:
                            pe.wait_ge(sem["gate_ready"], at("gate_ready", bf, 2 * t + c - 1))
                        for k in range(KT):
                            last = mm(psum[BANKS["G"]][:], xqT[:, k, t * P:(t + 1) * P], wg16[:, k, c * 512:(c + 1) * 512],
                                      start=k == 0, stop=k == KT - 1)
                        last.then_inc(sem["G_mm"], 1)
                    elif kind == "U":
                        t, c = args
                        if (t, c) == (0, 0):
                            pe.wait_ge(sem["pTx1_ready"], at("pTx1_ready", bf, 7))
                        else:
                            pe.wait_ge(sem["h_ready"], at("h_ready", bf, 2 * t + c - 1))
                        for k in range(KT):
                            last = mm(psum[BANKS["U"]][:], xqT[:, k, t * P:(t + 1) * P], wu16[:, k, c * 512:(c + 1) * 512],
                                      start=k == 0, stop=k == KT - 1)
                        last.then_inc(sem["U_mm"], 1)
                    elif kind == "HT":
                        t, = args
                        pe.wait_ge(sem["hq_ready"], at("hq_ready", bf, t))
                        if t:
                            pe.wait_ge(sem["hqT_ready"], at("hqT_ready", bf, 0))
                            if phase != "final":
                                pe.wait_ge(sem["qxT_ready"], at("qxT_ready", br))
                        elif phase != "final":
                            pe.wait_ge(sem["qx_raw"], at("qx_raw", br))
                        transposes16(psum[7], [hq[:, k * P:(k + 1) * P] for k in range(IC)]).then_inc(sem["HT_mm"], 1)
                    elif kind == "D":
                        pe.wait_ge(sem["hqT_ready"], at("hqT_ready", bf, 1))
                        for t in range(TT):
                            for k in range(IC):
                                last = mm(psum[7][:, t * D:(t + 1) * D], hqT[:, t, k, :], wd16[:, k, :],
                                          start=k == 0, stop=k == IC - 1)
                        last.then_inc(sem["D_mm"], 1)

            pe.wait_ge(pool_consts, POOL_CONSTS)
            pe.wait_ge(pre_dve, 4)
            run("first", None, None)
            pe.wait_ge(weights_loaded, N_LOADS)
            pe.wait_ge(pre_dve, 11)
            for n, w in enumerate((wqx, wkvx[:, :, 0:D], wkvx[:, :, D:2 * D], wox)):
                for k in range(KT):
                    mm(psum[1 + n // 2][:, (n % 2) * D:(n % 2 + 1) * D], bwide[:, n, k, :], w[:, k, :], start=k == 0, stop=k == KT - 1)
            mm(psum[0][:, 0:3], ones, wsum[:], start=True, stop=True).then_inc(pre_pe, 1)
            pe.wait_ge(pre_dve, PRE_DVE)
            run("second", 0, -1)
            run("third", 1, 0)
            with pe.Fori(0, B - 3) as j:
                run("body", j + 2, j + 1)
            run("next_to_last", B - 1, B - 2)
            run("last", None, B - 1)
            run("final", None, B)

        @block.vector
        def _(dve):
            v = nc.vector

            def ln_stats(n, b):
                for t in range(TT):
                    v.bn_stats(bn[:, n, t, :], LN[n][:, t, :]).then_inc(sem["ln_stats"], 1)
                for t in range(TT):
                    dve.wait_ge(sem["ln_stats"], at("ln_stats", b, 2 * n + t))
                    dve.sem_inc(waits_passed, 1)
                    v.bn_aggr(mv[:, n, t, :], bn[:, n, t, :]).then_inc(sem["ln_mv"], 1)

            def ln_apply(n, b, dst, done):
                dve.wait_ge(sem["ln_rstd"], at("ln_rstd", b, n))
                for t in range(TT):
                    v.tensor_scalar(dst[:, t, :], LN[n][:, t, :], mv[:, n, t, 0:1], rstd[:, n, t:t + 1],
                                    ALU.subtract, ALU.mult).then_inc(done, 1)

            def turn_x(n, src, b):
                sine = ropex[:, n, 1, :, :].unsqueeze(2).to_broadcast([P, TT, XH, XD])
                four = src[:].rearrange("p t (h d) -> p t h d", h=XH)
                dst = turn[n][:, 1, :, :].rearrange("p t (h d) -> p t h d", h=XH)
                for odd in range(2):
                    v.tensor_tensor(dst[:, :, :, odd::2], four[:, :, :, 1 - odd::2], sine[:, :, :, odd::2], ALU.mult)\
                        .then_inc(sem["turned"], 1)

            def quant_h(b, t):
                dve.wait_ge(sem["h_ready"], at("h_ready", b, 2 * t + 1))
                v.tensor_reduce(hs[:, 0, t:t + 1], hh[:, t, :], AX_X, ALU.max, apply_absolute_value=True).then_inc(sem["quant_h"], 1)
                dve.wait_ge(sem["quant_h"], at("quant_h", b, 5 * t))
                v.tensor_scalar(hs[:, 1, t:t + 1], hs[:, 0, t:t + 1], ax[:, 6, t:t + 1], EPS, ALU.mult, ALU.max).then_inc(sem["quant_h"], 1)
                dve.wait_ge(sem["quant_h"], at("quant_h", b, 5 * t + 1))
                v.reciprocal(hs[:, 2, t:t + 1], hs[:, 1, t:t + 1]).then_inc(sem["quant_h"], 1)
                dve.wait_ge(sem["quant_h"], at("quant_h", b, 5 * t + 2))
                v.tensor_scalar(hs[:, 3, t:t + 1], hs[:, 2, t:t + 1], 127.0, ax[:, 6, t:t + 1], ALU.mult, ALU.mult).then_inc(sem["quant_h"], 1)
                dve.wait_ge(sem["quant_h"], at("quant_h", b, 5 * t + 3))
                v.tensor_scalar(hh[:, t, :], hh[:, t, :], hs[:, 3, t:t + 1], MAGIC, ALU.mult, ALU.add).then_inc(sem["hq_shift"], 1)
                v.tensor_scalar(hs[:, 5, t:t + 1], hs[:, 1, t:t + 1], 1.0 / 127.0, wk1[:, 2:3], ALU.mult, ALU.mult).then_inc(sem["quant_h"], 1)
                dve.wait_ge(sem["hq_shift"], at("hq_shift", b, t))
                dve.wait_ge(sem["HT_mm"], at("HT_mm", b, t - 1))
                v.tensor_scalar(hq[:], hh[:, t, :], MAGIC, 127.0, ALU.subtract, ALU.min).then_inc(sem["hq_ready"], 1)

            def run(phase, bm, br):
                head = phase in ("second", "third", "body")
                bh = 0 if phase == "first" else bm + 1 if head else None
                ahead = phase in ("second", "third", "body", "next_to_last")
                bk = br + 1 if ahead else None
                bf = None if phase == "first" else br - 1
                for step in STEPS[phase]:
                    kind, args = step[0], step[1:]
                    if kind == "X":
                        dve.wait_ge(sem["x_hi"], at("x_hi", bh))
                        v.tensor_tensor(x_lo[:], xT[:], x_hi[:].bitcast(F32), ALU.subtract).then_inc(sem["x_lo"], 1)
                    elif kind == "proj":
                        t, c = args
                        b = bm if c == 2 else bh
                        n = 2 * c + t
                        heads = 8 if c else KV
                        bank = psum[BANKS["proj"]][:, 0:heads * HD].rearrange("p (h a n) -> p h a n", h=heads, a=2)
                        cosine = rope[:, 0, t:t + 1, :].to_broadcast([P, heads, HD])
                        sine = rope[:, 1, t:t + 1, :].to_broadcast([P, heads, HD])
                        by_cos = rot[:, n % 2, 0:heads * HD].rearrange("p (h n) -> p h n", h=heads)
                        by_sin = rot[:, 2, 0:heads * HD].rearrange("p (h n) -> p h n", h=heads)
                        dve.wait_ge(sem["proj_mm"], at("proj_mm", b, n))
                        dve.wait_ge(sem["rot_lo"], at("rot_lo", b, n - 2))
                        v.tensor_tensor(by_cos, psum[BANKS["proj"]][:, 0:heads * HD].rearrange("p (h n) -> p h n", h=heads), cosine,
                                        ALU.mult).then_inc(sem["rot_prod"], 1)
                        dve.wait_ge(sem["rot_sum"], at("rot_sum", b, n - 1))
                        for a_ in range(2):
                            lo = a_ * HD // 2
                            v.tensor_tensor(by_sin[:, :, lo:lo + HD // 2], bank[:, :, 1 - a_, :], sine[:, :, lo:lo + HD // 2],
                                            ALU.mult).then_inc(sem["rot_prod"], 1)
                        if c == 0:
                            dve.wait_ge(sem["v_ready"], at("v_ready", b - 1))
                            v.tensor_copy(v_new[:, t, :], psum[BANKS["proj"]][:, KV * HD:2 * KV * HD]).then_inc(sem["v_new"], 1)
                    elif kind == "S":
                        p, q = args
                        n = 2 * p + q
                        dve.wait_ge(sem["S_mm"], at("S_mm", bm, n))
                        dve.sem_inc(waits_passed, 1)
                        for c in range(2):
                            v.tensor_tensor_reduce(out=prob[:, n % 4, c, :], in0=psum[BANKS["S"][n % 2]][:, c * L:(c + 1) * L],
                                                   in1=alibi[:, c, :], scale=-2.0 ** -p, scalar=3.0e38,
                                                   op0=ALU.add, op1=ALU.min, accum_out=nmax[:, 2 * n + c:2 * n + c + 1])\
                                .then_inc(sem["s_neg"], 1)
                    elif kind == "R":
                        p, q = args
                        n = 2 * p + q
                        dve.wait_ge(sem["p_exp"], at("p_exp", bm, 2 * n + 1))
                        v.reciprocal(precs[:, 2 * n:2 * n + 2], psums[:, 2 * n:2 * n + 2]).then_inc(sem["p_recip"], 1)
                    elif kind == "W":
                        dve.wait_ge(sem["xtok_loaded"], landed("xtok_loaded", br))
                        dve.wait_ge(sem["W_mm"], at("W_mm", br))
                        v.tensor_tensor(y[:], psum[BANKS["W"]][:].rearrange("p (t n) -> p t n", t=TT), xtok[:], ALU.add)\
                            .then_inc(sem["y_ready"], 1)
                    elif kind == "y_stats":
                        dve.wait_ge(sem["y_ready"], at("y_ready", br))
                        ln_stats(LN_Y, br)
                    elif kind == "ctx_stats":
                        dve.wait_ge(sem["ctx_loaded"], landed("ctx_loaded", bk))
                        for t in range(TT):
                            v.bn_stats(bn[:, LN_CTX, t, :], ctxt[:, t, :]).then_inc(sem["ctx_stats"], 1)
                        for t in range(TT):
                            dve.wait_ge(sem["ctx_stats"], at("ctx_stats", bk, t))
                            dve.sem_inc(waits_passed, 1)
                            v.bn_aggr(mv[:, LN_CTX, t, :], bn[:, LN_CTX, t, :]).then_inc(sem["ctx_mv"], 1)
                    elif kind == "y_apply":
                        ln_apply(LN_Y, br, x1, sem["x1_ready"])
                        dve.wait_ge(sem["x1_ready"], at("x1_ready", br, 1))
                        ln_stats(LN_X1, br)
                    elif kind == "ctx_apply":
                        dve.wait_ge(sem["ctx_rstd"], at("ctx_rstd", bk))
                        for t in range(TT):
                            v.tensor_scalar(ncx[:, t, :], ctxt[:, t, :], mv[:, LN_CTX, t, 0:1], rstd[:, LN_CTX, t:t + 1],
                                            ALU.subtract, ALU.mult).then_inc(sem["nc_ready"], 1)
                    elif kind == "x1_apply":
                        dve.wait_ge(sem["KXT_mm"], at("KXT_mm", br))
                        ln_apply(LN_X1, br, nx, sem["nx_ready"])
                    elif kind == "mask":
                        dve.wait_ge(sem["cell_loaded"], landed("cell_loaded", bk))
                        v.tensor_copy(cellqf[:], cellq[:]).then_inc(sem["cellq_ready"], 1)
                        dve.wait_ge(sem["cellq_ready"], at("cellq_ready", bk))
                        v.scalar_tensor_tensor(out=pm0[:], in0=cellk[:, 0:P], scalar=cellqf[:, 0:1], in1=pen0[:],
                                               op0=ALU.not_equal, op1=ALU.max).then_inc(sem["pen_ready"], 1)
                        v.scalar_tensor_tensor(out=pm1[:], in0=cellk[:, WIN:L], scalar=cellqf[:, 1:2], in1=pen1[:],
                                               op0=ALU.not_equal, op1=ALU.max).then_inc(sem["pen_ready"], 1)
                        dve.wait_ge(sem["pen_ready"], at("pen_ready", bk, 1))
                        v.tensor_scalar(mask0[:], pm0[:], -BIG, None, ALU.mult).then_inc(sem["mask_ready"], 1)
                        v.tensor_scalar(mask1[:], pm1[:], -BIG, None, ALU.mult).then_inc(sem["mask_ready"], 1)
                    elif kind == "KV":
                        t, = args
                        dve.wait_ge(sem["KV_mm"], at("KV_mm", bk, t))
                        v.tensor_tensor(kx_tok[:, t, :], psum[7][:, 0:D], brow[:, 1, :], ALU.add).then_inc(sem["kx_raw"], 1)
                        v.tensor_tensor(vx[:, t, :, 0:XD], psum[7][:, D:2 * D].rearrange("p (h n) -> p h n", h=XH),
                                        brow[:, 2, :].rearrange("p (h n) -> p h n", h=XH), ALU.add).then_inc(sem["vx_ready"], 1)
                    elif kind == "k_turn":
                        dve.wait_ge(sem["kx_raw"], at("kx_raw", bk, 1))
                        turn_x(0, kx_tok, bk)
                    elif kind == "QX":
                        dve.wait_ge(sem["QX_mm"], at("QX_mm", br))
                        v.tensor_tensor(qx_tok[:], psum[7][:].rearrange("p (t n) -> p t n", t=TT),
                                        brow[:, 0:1, :].to_broadcast([P, TT, D]), ALU.add).then_inc(sem["qx_raw"], 1)
                    elif kind == "q_turn":
                        dve.wait_ge(sem["qx_raw"], at("qx_raw", br))
                        turn_x(1, qx_tok, br)
                    elif kind == "SX0":
                        t, = args
                        if t == 0:
                            dve.wait_ge(sem["mask_ready"], at("mask_ready", br, 1))
                        dve.wait_ge(sem["SX0_mm"], at("SX0_mm", br, t))
                        dve.sem_inc(waits_passed, 1)
                        for h in range(4):
                            v.tensor_tensor_reduce(out=px0[:, t % 2, h, :], in0=psum[BANKS["SX"]][:, h * P:(h + 1) * P],
                                                   in1=mask0[:], scale=-1.0, scalar=3.0e38, op0=ALU.add, op1=ALU.min,
                                                   accum_out=nmx[:, 0, 4 * t + h:4 * t + h + 1]).then_inc(sem["sx0_neg"], 1)
                    elif kind == "SX1":
                        t, hf = args
                        n = 2 * t + hf
                        dve.wait_ge(sem["SX1_mm"], at("SX1_mm", br, n))
                        dve.sem_inc(waits_passed, 1)
                        for c in range(2):
                            h = 4 * t + 2 * hf + c
                            v.tensor_tensor_reduce(out=px1[:, n % 3, c, WIN:L], in0=psum[BANKS["SX"]][:, c * K1:(c + 1) * K1],
                                                   in1=mask1[:], scale=-1.0, scalar=3.0e38, op0=ALU.add, op1=ALU.min,
                                                   accum_out=nmx[:, 1, h:h + 1]).then_inc(sem["sx1_neg"], 1)
                    elif kind == "TX0":
                        t, = args
                        dve.wait_ge(sem["TX0_mm"], at("TX0_mm", br, t))
                        v.tensor_copy(pTx[:, t % 2, :, 0, :], psum[BANKS["TX"]][:].rearrange("p (h n) -> p h n", h=4))\
                            .then_inc(sem["pTx0_ready"], 1)
                    elif kind == "BX":
                        q, = args
                        if q == 0:
                            dve.wait_ge(sem["px0_exp"], at("px0_exp", br, 15))
                        else:
                            dve.wait_ge(sem["px1_exp"], at("px1_exp", br, 15))
                        v.reciprocal(recx[:, q, :], sumx[:, q, :]).then_inc(sem["sx_recip"], 1)
                        dve.wait_ge(sem["BX_mm"], at("BX_mm", br, q))
                        dve.wait_ge(sem["sx_recip"], at("sx_recip", br, q))
                        v.tensor_tensor(o_tok[:, q, :].rearrange("p (h n) -> p h n", h=XH),
                                        psum[7][:].rearrange("p (h n) -> p h n", h=XH)[:, :, 0:XD],
                                        recx[:, q, :].unsqueeze(2).to_broadcast([P, XH, XD]), ALU.mult)\
                            .then_inc(sem["o_ready"], 1)
                    elif kind == "o_stats":
                        dve.wait_ge(sem["o_ready"], at("o_ready", br, 1))
                        ln_stats(LN_O, br)
                    elif kind == "o_apply":
                        dve.wait_ge(sem["NX_mm"], at("NX_mm", br))
                        ln_apply(LN_O, br, n_o, sem["no_ready"])
                    elif kind == "PO":
                        dve.wait_ge(sem["PO_mm"], at("PO_mm", br))
                        dve.wait_ge(sem["x1b_ready"], at("x1b_ready", br))
                        v.tensor_tensor(y2[:], psum[7][:].rearrange("p (t n) -> p t n", t=TT), x1[:], ALU.add)\
                            .then_inc(sem["y2_ready"], 1)
                    elif kind == "y2_stats":
                        dve.wait_ge(sem["y2_ready"], at("y2_ready", br))
                        ln_stats(LN_Y2, br)
                    elif kind == "y2_apply":
                        ln_apply(LN_Y2, br, x2, sem["x2_ready"])
                    elif kind == "quant_x":
                        dve.wait_ge(sem["x2_ready"], at("x2_ready", bf, 1))
                        v.tensor_reduce(amx[:], x2[:], AX_X, ALU.max, apply_absolute_value=True).then_inc(sem["quant_x"], 1)
                        dve.wait_ge(sem["quant_x"], at("quant_x", bf, 0))
                        v.tensor_scalar(ax[:, 0, :], amx[:], EPS, None, ALU.max).then_inc(sem["quant_x"], 1)
                        dve.wait_ge(sem["quant_x"], at("quant_x", bf, 1))
                        v.reciprocal(ax[:, 1, :], ax[:, 0, :]).then_inc(sem["quant_x"], 1)
                        dve.wait_ge(sem["quant_x"], at("quant_x", bf, 2))
                        v.tensor_scalar(ax[:, 2, :], ax[:, 1, :], 127.0, None, ALU.mult).then_inc(sem["quant_x"], 1)
                        dve.wait_ge(sem["quant_x"], at("quant_x", bf, 3))
                        for t in range(TT):
                            v.tensor_scalar(xshift[:, t, :], x2[:, t, :], ax[:, 2, t:t + 1], MAGIC, ALU.mult, ALU.add)\
                                .then_inc(sem["xq_shift"], 1)
                        v.tensor_scalar(ax[:, 3, :], ax[:, 0, :], 1.0 / 127.0, None, ALU.mult).then_inc(sem["quant_x"], 1)
                        dve.wait_ge(sem["xq_shift"], at("xq_shift", bf, 1))
                        dve.wait_ge(sem["HT_mm"], at("HT_mm", bf - 1, 1))
                        v.tensor_scalar(xq, xshift, MAGIC, 127.0, ALU.subtract, ALU.min).then_inc(sem["xq_ready"], 1)
                        dve.wait_ge(sem["tanh_ready"], at("tanh_ready", bf - 1, 3))
                        dve.wait_ge(sem["quant_x"], at("quant_x", bf, 4))
                        v.tensor_scalar(ax[:, 4, :], ax[:, 3, :], wk1[:, 0:1], None, ALU.mult).then_inc(sem["xs_tanh"], 1)
                        v.tensor_tensor(ax[:, 5, :], ax[:, 3, :], ax[:, 3, :], ALU.mult).then_inc(sem["quant_x"], 1)
                        dve.wait_ge(sem["quant_x"], at("quant_x", bf, 5))
                        v.tensor_scalar(ax[:, 6, :], ax[:, 5, :], wk1[:, 1:2], None, ALU.mult).then_inc(sem["xs_half"], 1)
                    elif kind == "XQ":
                        dve.wait_ge(sem["XQ_mm"], at("XQ_mm", bf))
                        dve.wait_ge(sem["U_mm"], at("U_mm", bf - 1, 3))
                        v.tensor_scalar(xqT[:], psum[7][:].bitcast(BF16)[:, 0:KT * L].rearrange("p (k n) -> p k n", k=KT),
                                        -128.0, None, ALU.max).then_inc(sem["xqT_ready"], 1)
                    elif kind == "U":
                        t, c = args
                        n = 2 * t + c
                        part = hh[:, t, c * 512:(c + 1) * 512]
                        dve.wait_ge(sem["tanh_ready"], at("tanh_ready", bf, n))
                        v.scalar_tensor_tensor(out=part, in0=part, scalar=1.0, in1=psum[BANKS["G"]][:], op0=ALU.add, op1=ALU.mult)\
                            .then_inc(sem["gate_ready"], 1)
                        dve.wait_ge(sem["gate_ready"], at("gate_ready", bf, n))
                        dve.wait_ge(sem["U_mm"], at("U_mm", bf, n))
                        v.tensor_tensor(part, part, psum[BANKS["U"]][:], ALU.mult).then_inc(sem["h_ready"], 1)
                    elif kind == "quant_h":
                        t, = args
                        quant_h(bf, t)
                    elif kind == "HT":
                        t, = args
                        dve.wait_ge(sem["HT_mm"], at("HT_mm", bf, t))
                        dve.wait_ge(sem["D_mm"], at("D_mm", bf - 1))
                        v.tensor_scalar(hqT[:, t, :, :], psum[7][:].bitcast(BF16).rearrange("p (k n) -> p k n", k=IC),
                                        -128.0, None, ALU.max).then_inc(sem["hqT_ready"], 1)
                    elif kind == "D":
                        dve.wait_ge(sem["stored"], landed("stored", bf - 1))
                        dve.wait_ge(sem["D_mm"], at("D_mm", bf))
                        for t in range(TT):
                            v.scalar_tensor_tensor(out=y3[:, t, :], in0=psum[7][:, t * D:(t + 1) * D], scalar=hs[:, 5, t:t + 1],
                                                   in1=x2[:, t, :], op0=ALU.mult, op1=ALU.add).then_inc(sem["y3_ready"], 1)
                    elif kind == "y3_stats":
                        dve.wait_ge(sem["y3_ready"], at("y3_ready", bf, 1))
                        for t in range(TT):
                            v.bn_stats(bn[:, LN_Y3, t, :], y3[:, t, :]).then_inc(sem["y3_stats"], 1)
                        for t in range(TT):
                            dve.wait_ge(sem["y3_stats"], at("y3_stats", bf, t))
                            dve.sem_inc(waits_passed, 1)
                            v.bn_aggr(mv[:, LN_Y3, t, :], bn[:, LN_Y3, t, :]).then_inc(sem["y3_mv"], 1)
                    elif kind == "y3_apply":
                        dve.wait_ge(sem["y3_rstd"], at("y3_rstd", bf))
                        for t in range(TT):
                            v.tensor_scalar(y3[:, t, :], y3[:, t, :], mv[:, LN_Y3, t, 0:1], rstd[:, LN_Y3, t:t + 1],
                                            ALU.subtract, ALU.mult).then_inc(sem["out_ready"], 1)

            dve.wait_ge(proj_loaded, 16 * len(first_loads))
            for k in range(KT):
                v.tensor_copy(w_hi[:, k, :], raw_w[k]).then_inc(pre_dve, 1)
            for k in range(KT):
                dve.wait_ge(pre_dve, k + 1)
                v.tensor_tensor(w_lo[:, k, :], raw_w[k], w_hi[:, k, :].bitcast(F32), ALU.subtract).then_inc(pre_dve, 1)
            run("first", None, None)
            dve.wait_ge(weights_loaded, N_LOADS)
            for n in range(4):
                v.tensor_copy(bwide[:, n, :, :], gb[:, 2 * n + 1, :].unsqueeze(2).to_broadcast([P, KT, P])).then_inc(pre_dve, 1)
            for n in range(3):
                v.tensor_reduce(wsum[:, n:n + 1], stage[n], AX_X, ALU.add, apply_absolute_value=True).then_inc(pre_dve, 1)
            dve.wait_ge(pre_pe, 1)
            for n in range(2):
                v.tensor_tensor(brow[:, 2 * n:2 * n + 2, :], psum[1 + n][:].rearrange("p (c n) -> p c n", c=2),
                                brow[:, 2 * n:2 * n + 2, :], ALU.add).then_inc(pre_dve, 1)
            for w, col in ((wqx, 0), (wkvx[:, :, 0:D], 2), (wkvx[:, :, D:2 * D], 4), (wox, 6)):
                for k in range(KT):
                    v.tensor_scalar(w[:, k, :], w[:, k, :], gb[:, col, k:k + 1], None, ALU.mult).then_inc(pre_dve, 1)
            v.tensor_scalar(wmean[:], psum[0][:, 0:3], 1.0 / (INNER * D), EPS, ALU.mult, ALU.max).then_inc(pre_dve, 1)
            dve.wait_ge(pre_dve, 22)
            v.reciprocal(wrec[:], wmean[:]).then_inc(pre_dve, 1)
            v.tensor_scalar(wk1[:, 0:1], wmean[:, 0:1], 0.5, None, ALU.mult).then_inc(pre_dve, 1)
            v.tensor_tensor(wk1[:, 2:3], wmean[:, 2:3], ones[:, 0:1], ALU.mult).then_inc(pre_dve, 1)
            dve.wait_ge(pre_dve, 25)
            v.tensor_tensor(wk1[:, 1:2], wk1[:, 0:1], wmean[:, 1:2], ALU.mult).then_inc(pre_dve, 1)
            for n in range(3):
                v.tensor_scalar(stage[n], stage[n], wrec[:, n:n + 1], MAGIC, ALU.mult, ALU.add).then_inc(pre_dve, 1)
            for n in range(3):
                dve.wait_ge(pre_dve, 27 + n)
                v.tensor_scalar(stage[n], stage[n], MAGIC, 1.0, ALU.subtract, ALU.min).then_inc(pre_dve, 1)
            for n, dst in enumerate((wg16, wu16, wd16)):
                dve.wait_ge(pre_dve, 30 + n)
                v.tensor_scalar(dst[:].rearrange("p k n -> p (k n)"), stage[n], -1.0, None, ALU.max).then_inc(pre_dve, 1)
            dve.wait_ge(pre_dve, PRE_DVE)
            dve.wait_ge(pool_consts, POOL_CONSTS)
            run("second", 0, -1)
            run("third", 1, 0)
            with dve.Fori(0, B - 3) as j:
                run("body", j + 2, j + 1)
            run("next_to_last", B - 1, B - 2)
            run("last", None, B - 1)
            run("final", None, B)

        @block.scalar
        def _(act):
            def run(phase, bm, br):
                head = phase in ("second", "third", "body")
                bh = 0 if phase == "first" else bm + 1 if head else None
                ahead = phase in ("second", "third", "body", "next_to_last")
                bk = br + 1 if ahead else None
                bf = None if phase == "first" else br - 1
                for step in STEPS[phase]:
                    kind, args = step[0], step[1:]
                    if kind == "X":
                        act.wait_ge(sem["xT_loaded"], landed("xT_loaded", bh))
                        act.wait_ge(sem["proj_mm"], at("proj_mm", bh - 1, 5))
                        nc.scalar.copy(x_hi[:], xT[:]).then_inc(sem["x_hi"], 1)
                    elif kind == "proj":
                        t, c = args
                        b = bm if c == 2 else bh
                        n = 2 * c + t
                        act.wait_ge(sem["rot_sum"], at("rot_sum", b, n))
                        if c == 0:
                            nc.scalar.copy(ktok[:, t, :, :].rearrange("p g (a n) -> p g a n", a=3)[:, :, 0::2, :],
                                           rot[:, n % 2, 0:KV * HD].rearrange("p (g a n) -> p g a n", g=KV, a=1)
                                           .to_broadcast([P, KV, 2, HD])).then_inc(sem["rot_hi"], 1)
                        else:
                            nc.scalar.copy(qtok[:, t, :, 0:HD], rot[:, n % 2, :].rearrange("p (h n) -> p h n", h=8))\
                                .then_inc(sem["rot_hi"], 1)
                    elif kind == "kT":
                        i, = args
                        t, h = i % 2, i // 2
                        act.wait_ge(sem["kT_mm"], at("kT_mm", bh, i))
                        nc.scalar.copy(kk[:, :, 2 * h:2 * h + 2, t * P:(t + 1) * P].rearrange("p c g n -> p g c n"),
                                       psum[BANKS["kT"]][:].rearrange("p (g c n) -> p g c n", g=2, c=2)).then_inc(sem["k_ready"], 1)
                    elif kind == "qT":
                        p, = args
                        b = bh if p < 2 else bm
                        act.wait_ge(sem["qT_mm"], at("qT_mm", b, p))
                        nc.scalar.activation(qq[:, p % 3, :, :], psum[BANKS["qT"]][:].rearrange("p (c n) -> p c n", c=2), ACT.Copy,
                                             scale=2.0 ** p / 8.0).then_inc(sem["q_ready"], 1)
                    elif kind == "S":
                        p, q = args
                        n = 2 * p + q
                        for c in range(2):
                            i = 2 * n + c
                            act.wait_ge(sem["s_neg"], at("s_neg", bm, i))
                            nc.scalar.activation(prob[:, n % 4, c, :], prob[:, n % 4, c, :], ACT.Exp,
                                                 bias=nmax[:, i:i + 1], scale=-1.0, accum_out=psums[:, i:i + 1])\
                                .then_inc(sem["p_exp"], 1)
                    elif kind == "T":
                        p, q = args
                        act.wait_ge(sem["T_mm"], at("T_mm", bm, 2 * p + q))
                        nc.scalar.copy(pT[:, p % 2, :, :, q * P:(q + 1) * P].rearrange("p c k n -> p (c k) n"),
                                       psum[BANKS["T"]][:].rearrange("p (c n) -> p c n", c=4)).then_inc(sem["pT_ready"], 1)
                    elif kind == "O":
                        u, = args
                        act.wait_ge(sem["O_mm"], at("O_mm", bm, u))
                        nc.scalar.copy(oT[:, u, :], psum[BANKS["O"]][:, 0:L]).then_inc(sem["oT_ready"], 1)
                    elif kind == "C":
                        act.wait_ge(sem["C_mm"], at("C_mm", bk))
                        act.wait_ge(sem["KV_mm"], at("KV_mm", bk - 1, 1))
                        nc.scalar.copy(cT[:], psum[7][:].rearrange("p (k n) -> p k n", k=KT)).then_inc(sem["cT_ready"], 1)
                    elif kind == "NX":
                        act.wait_ge(sem["NX_mm"], at("NX_mm", br))
                        act.wait_ge(sem["PO_mm"], at("PO_mm", br - 1))
                        nc.scalar.copy(nT[:], psum[7][:].rearrange("p (k n) -> p k n", k=KT)).then_inc(sem["nT_ready"], 1)
                    elif kind == "NO":
                        act.wait_ge(sem["NO_mm"], at("NO_mm", br))
                        act.wait_ge(sem["QX_mm"], at("QX_mm", br))
                        nc.scalar.copy(noT[:], psum[7][:].rearrange("p (k n) -> p k n", k=KT)).then_inc(sem["noT_ready"], 1)
                    elif kind == "KXT":
                        act.wait_ge(sem["KXT_mm"], at("KXT_mm", bk))
                        act.wait_ge(sem["kx_ready"], at("kx_ready", bk - 1, 3))
                        nc.scalar.copy(kxT[:], psum[7][:].rearrange("p (k n) -> p k n", k=KT)).then_inc(sem["kxT_ready"], 1)
                    elif kind == "QXT":
                        act.wait_ge(sem["QXT_mm"], at("QXT_mm", br))
                        act.wait_ge(sem["SX1_mm"], at("SX1_mm", br - 1, 7))
                        nc.scalar.copy(qx[:], psum[7][:].rearrange("p (k n) -> p k n", k=KT)).then_inc(sem["qxT_ready"], 1)
                    elif kind == "SX0":
                        t, = args
                        if t == 0:
                            act.wait_ge(sem["sx_recip"], at("sx_recip", br - 1, 1))
                        for h in range(4):
                            i = 4 * t + h
                            act.wait_ge(sem["sx0_neg"], at("sx0_neg", br, i))
                            nc.scalar.activation(px0[:, t % 2, h, :], px0[:, t % 2, h, :], ACT.Exp, bias=nmx[:, 0, i:i + 1],
                                                 scale=-1.0, accum_out=sumx[:, 0, i:i + 1]).then_inc(sem["px0_exp"], 1)
                    elif kind == "SX1":
                        t, hf = args
                        n = 2 * t + hf
                        for c in range(2):
                            i = 2 * n + c
                            act.wait_ge(sem["sx1_neg"], at("sx1_neg", br, i))
                            nc.scalar.activation(px1[:, n % 3, c, WIN:L], px1[:, n % 3, c, WIN:L], ACT.Exp,
                                                 bias=nmx[:, 1, i:i + 1], scale=-1.0, accum_out=sumx[:, 1, i:i + 1])\
                                .then_inc(sem["px1_exp"], 1)
                    elif kind == "TX1":
                        t, hf = args
                        act.wait_ge(sem["TX1_mm"], at("TX1_mm", br, 2 * t + hf))
                        for c in range(2):
                            ins = nc.scalar.copy(pTx[:, t % 2, 2 * hf + c, 1:3, :],
                                                 psum[BANKS["TX"]][:, c * L:(c + 1) * L].rearrange("p (k n) -> p k n", k=TT))
                        ins.then_inc(sem["pTx1_ready"], 1)
                    elif kind == "OX":
                        u, = args
                        act.wait_ge(sem["OX_mm"], at("OX_mm", br, u))
                        nc.scalar.copy(ox[:, u, :], psum[7][:, 0:L]).then_inc(sem["ox_ready"], 1)
                    elif kind == "G":
                        t, c = args
                        n = 2 * t + c
                        if n == 0:
                            act.wait_ge(sem["xs_tanh"], at("xs_tanh", bf))
                        act.wait_ge(sem["G_mm"], at("G_mm", bf, n))
                        nc.scalar.activation(hh[:, t, c * 512:(c + 1) * 512], psum[BANKS["G"]][:], ACT.Tanh, scale=ax[:, 4, t:t + 1])\
                            .then_inc(sem["tanh_ready"], 1)

            run("first", None, None)
            run("second", 0, -1)
            run("third", 1, 0)
            with act.Fori(0, B - 3) as j:
                run("body", j + 2, j + 1)
            run("next_to_last", B - 1, B - 2)
            run("last", None, B - 1)
            run("final", None, B)

        @block.gpsimd
        def _(pool):
            g = nc.gpsimd

            def ln_rstd(b, n):
                pool.wait_ge(sem["ln_mv"], at("ln_mv", b, 2 * n + 1))
                pool.sem_inc(waits_passed, 1)
                g.tensor_scalar(veps[:, n, :], mv[:, n, :, 1], EPS, None, ALU.add).then_inc(sem["ln_eps"], 1)
                pool.wait_ge(sem["ln_eps"], at("ln_eps", b, n))
                g.tensor_tensor(rstd[:, n, :], veps[:, n, :], minus_half[:], ALU.pow).then_inc(sem["ln_rstd"], 1)

            def cosine_x(n, src):
                for t in range(TT):
                    ins = g.tensor_tensor(turn[n][:, 0, t, :].rearrange("p (h d) -> p h d", h=XH), src[:, t, :].rearrange("p (h d) -> p h d", h=XH),
                                          ropex[:, n, 0, t:t + 1, :].to_broadcast([P, XH, XD]), ALU.mult)
                ins.then_inc(sem["cosine"], 1)

            def run(phase, bm, br):
                head = phase in ("second", "third", "body")
                bh = 0 if phase == "first" else bm + 1 if head else None
                ahead = phase in ("second", "third", "body", "next_to_last")
                bk = br + 1 if ahead else None
                bf = None if phase == "first" else br - 1
                for step in STEPS[phase]:
                    kind, args = step[0], step[1:]
                    if kind == "proj":
                        t, c = args
                        b = bm if c == 2 else bh
                        n = 2 * c + t
                        width = 512 if c else KV * HD
                        total = rot[:, n % 2, 0:width]
                        pool.wait_ge(sem["rot_prod"], at("rot_prod", b, 3 * n + 2))
                        g.tensor_tensor(total, total, rot[:, 2, 0:width], ALU.add).then_inc(sem["rot_sum"], 1)
                        pool.wait_ge(sem["rot_hi"], at("rot_hi", b, n))
                        if c == 0:
                            g.tensor_tensor(ktok[:, t, :, HD:2 * HD], total.rearrange("p (g n) -> p g n", g=KV),
                                            ktok[:, t, :, 0:HD].bitcast(F32), ALU.subtract).then_inc(sem["rot_lo"], 1)
                        else:
                            g.tensor_tensor(qtok[:, t, :, HD:2 * HD], total.rearrange("p (h n) -> p h n", h=8),
                                            qtok[:, t, :, 0:HD].bitcast(F32), ALU.subtract).then_inc(sem["rot_lo"], 1)
                    elif kind == "V":
                        pool.wait_ge(sem["v_new"], at("v_new", bh, 1))
                        pool.wait_ge(sem["O_mm"], at("O_mm", bh - 1, PAIRS - 1))
                        pool.sem_inc(waits_passed, 1)
                        g.tensor_copy(v_sb[:], v_new[:]).then_inc(sem["v_ready"], 1)
                    elif kind == "R":
                        p, q = args
                        n = 2 * p + q
                        pool.wait_ge(sem["p_recip"], at("p_recip", bm, n))
                        g.tensor_tensor(prob[:, n % 4, :, :], prob[:, n % 4, :, :],
                                        precs[:, 2 * n:2 * n + 2].unsqueeze(2).to_broadcast([P, 2, L]), ALU.mult)\
                            .then_inc(sem["p_norm"], 1)
                    elif kind == "y_stats":
                        ln_rstd(br, LN_Y)
                    elif kind == "ctx_stats":
                        pool.wait_ge(sem["ctx_mv"], at("ctx_mv", bk, 1))
                        pool.sem_inc(waits_passed, 1)
                        g.tensor_scalar(veps[:, LN_CTX, :], mv[:, LN_CTX, :, 1], EPS, None, ALU.add).then_inc(sem["ctx_eps"], 1)
                        pool.wait_ge(sem["ctx_eps"], at("ctx_eps", bk))
                        g.tensor_tensor(rstd[:, LN_CTX, :], veps[:, LN_CTX, :], minus_half[:], ALU.pow).then_inc(sem["ctx_rstd"], 1)
                    elif kind == "y_apply":
                        ln_rstd(br, LN_X1)
                    elif kind == "o_stats":
                        ln_rstd(br, LN_O)
                    elif kind == "y2_stats":
                        ln_rstd(br, LN_Y2)
                    elif kind == "y3_stats":
                        pool.wait_ge(sem["y3_mv"], at("y3_mv", bf, 1))
                        pool.sem_inc(waits_passed, 1)
                        g.tensor_scalar(veps[:, LN_Y3, :], mv[:, LN_Y3, :, 1], EPS, None, ALU.add).then_inc(sem["y3_eps"], 1)
                        pool.wait_ge(sem["y3_eps"], at("y3_eps", bf))
                        g.tensor_tensor(rstd[:, LN_Y3, :], veps[:, LN_Y3, :], minus_half[:], ALU.pow).then_inc(sem["y3_rstd"], 1)
                    elif kind == "x1_apply":
                        pool.wait_ge(sem["nx_ready"], at("nx_ready", br, 1))
                        g.tensor_tensor(x1[:], x1[:], brow[:, 3:4, :].to_broadcast([P, TT, D]), ALU.add).then_inc(sem["x1b_ready"], 1)
                    elif kind == "k_turn":
                        pool.wait_ge(sem["kx_raw"], at("kx_raw", bk, 1))
                        cosine_x(0, kx_tok)
                        pool.wait_ge(sem["cosine"], at("cosine", bk, 0))
                        pool.wait_ge(sem["turned"], at("turned", bk, 1))
                        g.tensor_tensor(kx_tok[:], turn[0][:, 0, :, :], turn[0][:, 1, :, :], ALU.add).then_inc(sem["kx_rot"], 1)
                    elif kind == "q_turn":
                        pool.wait_ge(sem["qx_raw"], at("qx_raw", br))
                        cosine_x(1, qx_tok)
                        pool.wait_ge(sem["cosine"], at("cosine", br, 1))
                        pool.wait_ge(sem["turned"], at("turned", br, 3))
                        g.tensor_tensor(qx_tok[:], turn[1][:, 0, :, :], turn[1][:, 1, :, :], ALU.add).then_inc(sem["qx_rot"], 1)
                    elif kind == "KX":
                        t, = args
                        b = bk if t < 2 else br
                        if t == 0:
                            pool.wait_ge(sem["kxT_ready"], at("kxT_ready", b))
                        pool.wait_ge(sem["SX1_mm"], at("SX1_mm", b, 2 * (t - 2) + 1))
                        g.tensor_tensor(kx[:, t % 2, :, :], kxT[:, t // 2:t // 2 + 1, :].to_broadcast([P, 4, L]),
                                        own_head[:, 4 * (t % 2):4 * (t % 2) + 4].unsqueeze(2).to_broadcast([P, 4, L]), ALU.mult)\
                            .then_inc(sem["kx_ready"], 1)

            g.memset(ident[:], 0.0).then_inc(pool_consts, 1)
            g.memset(ident16[:], 0.0).then_inc(pool_consts, 1)
            g.memset(vx[:], 0.0).then_inc(pool_consts, 1)
            g.memset(px1[:], 0.0).then_inc(pool_consts, 1)
            g.memset(minus_half[:], -0.5).then_inc(pool_consts, 1)
            g.memset(ones, 1.0).then_inc(pool_consts, 1)
            pool.wait_ge(pool_consts, 6)
            for m in (ident, ident16):
                g.affine_select(out=m[:], in_=m[:], compare_op=ALU.not_equal, fill=1.0, base=0,
                                pattern=[[-1, P]], channel_multiplier=1).then_inc(pool_consts, 1)
            run("first", None, None)
            pool.wait_ge(pre_dve, PRE_DVE)
            run("second", 0, -1)
            run("third", 1, 0)
            with pool.Fori(0, B - 3) as j:
                run("body", j + 2, j + 1)
            run("next_to_last", B - 1, B - 2)
            run("last", None, B - 1)
            run("final", None, B)


def rope_table(n, dim, first, interleaved):
    inv = (np.float32(1.0) / np.power(np.float32(10000.0), np.arange(0, dim, 2, dtype=np.float32) / np.float32(dim))).astype(np.float32)
    freqs = (np.arange(first, first + n, dtype=np.float32)[:, None] * inv[None, :]).astype(np.float32)
    emb = np.repeat(freqs, 2, axis=-1) if interleaved else np.concatenate([freqs, freqs], axis=-1)
    emb = emb.astype(np.float64).T
    return np.cos(emb), np.sin(emb)


def by_token(table):
    return table.reshape(TT, P, -1).transpose(1, 0, 2).reshape(P, -1)


def constants():
    f = lambda x: np.ascontiguousarray(x, dtype=np.float32)
    cos, sin = rope_table(L, HD, 0, False)
    sgn = np.where(np.arange(HD) < HD // 2, -1.0, 1.0)
    rope = np.concatenate([by_token(cos.T), by_token(sin.T * sgn)], axis=1)
    slopes = np.array([(2.0 ** -0.5) ** (i + 1) for i in range(2)], dtype=np.float32)
    rel = (np.arange(L)[None, :] - np.arange(P)[:, None]).astype(np.float32)
    alibi = (slopes[:, None, None] * rel[None]).transpose(1, 0, 2).reshape(P, -1)
    sg = np.where(np.arange(XD) % 2 == 0, -1.0, 1.0)
    ropex = []
    for first, scale in ((WIN, 1.0), (0, 0.25)):
        cx, sx = rope_table(L, XD, first, True)
        ropex += [by_token(cx.T * scale), by_token(sx.T * sg * scale)]
    q, k = np.arange(L)[:, None], np.arange(L)[None, :]
    bad = ((k > q) | (k // WIN < q // WIN - 1)).astype(np.float32)
    own_head = np.repeat(np.eye(8), XD, axis=0)
    return dict(own_head=f(own_head), rope=f(rope), alibi=f(alibi), ropex=f(np.concatenate(ropex, axis=1)),
                pen0=f(bad[0:P, 0:P]), pen1=f(bad[P:, WIN:]))


def kernel(**inputs):
    import concourse.bacc as bacc
    from concourse.bass_utils import run_bass_kernel_spmd as launch

    t = {k: np.asarray(v) for k, v in inputs.items()}
    x = t["x"].reshape(B * L, D)
    xa = lambda n: t["L0_xattn_" + n]
    gb = np.stack([xa(f"ln_{n}_{c}").reshape(D) for n in "qkvo" for c in "wb"])
    arrays = dict(
        x=x, xT=x.T, ctx=t["ctx_1024"].reshape(B * L, D), cell=t["itok_Bx1xSx1_0_63"].reshape(B * L),
        wqkv=np.concatenate([t["L0_attn_Wk"], t["L0_attn_Wv"], t["L0_attn_Wq"]], axis=1), wo=t["L0_attn_Wo"],
        wqx=xa("w_q").T, wkvx=np.concatenate([xa("w_k").T, xa("w_v").T], axis=1), wox=xa("w_o").T,
        gb=gb.reshape(8, KT, P).transpose(2, 0, 1).reshape(P, 8 * KT),
        b_q=xa("b_q"), b_k=xa("b_k"), b_v=xa("b_v"), b_o=xa("b_o"),
        wg=t["L0_ffn_w_gate"].T, wu=t["L0_ffn_w_up"].T, wd=t["L0_ffn_w_down"].T,
        **constants(),
    )
    arrays = {k: np.ascontiguousarray(v) for k, v in arrays.items()}
    nc = bacc.Bacc("TRN2", target_bir_lowering=False, num_devices=1)
    aps = {k: nc.dram_tensor(f"in_{k}", v.shape, mybir.dt.from_np(v.dtype), kind="ExternalInput").ap() for k, v in arrays.items()}
    out = nc.dram_tensor("out_y", (B * L, D), F32, kind="ExternalOutput").ap()
    build(nc, aps, out)
    r = launch(nc, [{f"in_{k}": v for k, v in arrays.items()}], core_ids=[0])
    return r.results[0]["out_y"].reshape(B, L, D)
```
